# Optimizing a Trainium2 kernel written in Bass

```python
import numpy as np
import jax
import jax.numpy as jnp

def _softmax(x, axis=-1):
    return jax.nn.softmax(x, axis=axis)

def _gelu(x):
    return jax.nn.gelu(x, approximate=True)

def _silu(x):
    return jax.nn.silu(x)

def _sigmoid(x):
    return jax.nn.sigmoid(x)

def _layernorm(x, axis=-1, eps=1e-05):
    m = jnp.mean(x, axis=axis, keepdims=True)
    v = jnp.var(x, axis=axis, keepdims=True)
    return (x - m) / jnp.sqrt(v + eps)

def _scatter_add(tgt, idx, src, axis=0):
    return tgt.at[idx].add(src)

def _segment_sum(src, seg, n):
    return jax.ops.segment_sum(src, seg, n)
kernel_name = 'mk_seq_postln_d1_jaxref_r4_de4dec'

def setup_inputs(seed: int=0):
    np.random.seed(seed)
    _w = jnp.asarray

    def _L0_attn_setup():
        import jax, jax.numpy as jnp
        import numpy as np
        import math
        NUM_HEADS = 16
        DIM = 256
        DH = DIM // NUM_HEADS
        THETA = 10000.0
        SCALE_BASE = 512.0

        def _rotate_half(x):
            x = x.reshape(*x.shape[:-1], -1, 2)
            x1, x2 = (x[..., 0], x[..., 1])
            return jnp.stack((-x2, x1), axis=-1).reshape(*x1.shape[:-1], -1)

        def _xpos_rotate(q, k):
            s = q.shape[2]
            t = jnp.arange(s, dtype=jnp.float32)
            inv_freq = 1.0 / THETA ** (jnp.arange(0, DH, 2, dtype=jnp.float32) / DH)
            freqs = t[:, None] * inv_freq[None, :]
            freqs = jnp.repeat(freqs, 2, axis=-1)
            cos, sin = (jnp.cos(freqs), jnp.sin(freqs))
            base = (jnp.arange(0, DH, 2, dtype=jnp.float32) + 0.4 * DH) / (1.4 * DH)
            power = (t - s // 2) / SCALE_BASE
            scale = base[None, :] ** power[:, None]
            scale = jnp.concatenate((scale, scale), axis=-1)
            q = q * cos * scale + _rotate_half(q) * sin * scale
            inv_scale = 1.0 / scale
            k = k * cos * inv_scale + _rotate_half(k) * sin * inv_scale
            return (q, k)
        key = jax.random.key(seed)
        ks = jax.random.split(key, 5)
        b, s = (2, 512)
        w_scale = DIM ** (-0.5)
        return {'x': jax.random.normal(ks[0], (b, s, DIM), jnp.float32), 'Wq': jax.random.normal(ks[1], (DIM, DIM), jnp.float32) * w_scale, 'bq': jnp.zeros((DIM,), jnp.float32), 'Wk': jax.random.normal(ks[2], (DIM, DIM), jnp.float32) * w_scale, 'bk': jnp.zeros((DIM,), jnp.float32), 'Wv': jax.random.normal(ks[3], (DIM, DIM), jnp.float32) * w_scale, 'bv': jnp.zeros((DIM,), jnp.float32), 'Wo': jax.random.normal(ks[4], (DIM, DIM), jnp.float32) * w_scale, 'bo': jnp.zeros((DIM,), jnp.float32)}
    _L0_attn_in = _L0_attn_setup()

    def _L0_ffn_setup():
        import jax, jax.numpy as jnp
        import numpy as np
        DIM = 256
        INTER = 128
        E = 8
        TOP_K = 2
        ROUTE_SCALE = 1.0
        key = jax.random.key(seed)
        ks = jax.random.split(key, 8)
        s_d = 1.0 / np.sqrt(DIM)
        s_f = 1.0 / np.sqrt(INTER)
        x = jax.random.normal(ks[0], (2, 512, DIM), dtype=jnp.float32)
        gate_w = jax.random.uniform(ks[1], (E, DIM), jnp.float32, -s_d, s_d)
        wg = jax.random.uniform(ks[2], (E, INTER, DIM), jnp.float32, -s_d, s_d)
        wu = jax.random.uniform(ks[3], (E, INTER, DIM), jnp.float32, -s_d, s_d)
        wd = jax.random.uniform(ks[4], (E, DIM, INTER), jnp.float32, -s_f, s_f)
        sg = jax.random.uniform(ks[5], (INTER, DIM), jnp.float32, -s_d, s_d)
        su = jax.random.uniform(ks[6], (INTER, DIM), jnp.float32, -s_d, s_d)
        sd = jax.random.uniform(ks[7], (DIM, INTER), jnp.float32, -s_f, s_f)
        return {'x': x, 'gate_w': gate_w, 'wg': wg, 'wu': wu, 'wd': wd, 'sg': sg, 'su': su, 'sd': sd}
    _L0_ffn_in = _L0_ffn_setup()
    _d = {'L0_attn_x': _L0_attn_in['x'], 'L0_attn_Wq': _L0_attn_in['Wq'], 'L0_attn_bq': _L0_attn_in['bq'], 'L0_attn_Wk': _L0_attn_in['Wk'], 'L0_attn_bk': _L0_attn_in['bk'], 'L0_attn_Wv': _L0_attn_in['Wv'], 'L0_attn_bv': _L0_attn_in['bv'], 'L0_attn_Wo': _L0_attn_in['Wo'], 'L0_attn_bo': _L0_attn_in['bo'], 'L0_ffn_gate_w': _L0_ffn_in['gate_w'], 'L0_ffn_wg': _L0_ffn_in['wg'], 'L0_ffn_wu': _L0_ffn_in['wu'], 'L0_ffn_wd': _L0_ffn_in['wd'], 'L0_ffn_sg': _L0_ffn_in['sg'], 'L0_ffn_su': _L0_ffn_in['su'], 'L0_ffn_sd': _L0_ffn_in['sd']}
    _x0 = _d['L0_attn_x']
    _d['L0_attn_x'] = jax.random.normal(jax.random.fold_in(jax.random.key(seed), 1), (2, 2048, 256), dtype=_x0.dtype)
    del _x0
    return _d

def reference(L0_attn_x, L0_attn_Wq, L0_attn_bq, L0_attn_Wk, L0_attn_bk, L0_attn_Wv, L0_attn_bv, L0_attn_Wo, L0_attn_bo, L0_ffn_gate_w, L0_ffn_wg, L0_ffn_wu, L0_ffn_wd, L0_ffn_sg, L0_ffn_su, L0_ffn_sd):

    def _L0_attn_ref(x, Wq, bq, Wk, bk, Wv, bv, Wo, bo):
        import jax, jax.numpy as jnp
        import numpy as np
        import math
        NUM_HEADS = 16
        DIM = 256
        DH = DIM // NUM_HEADS
        THETA = 10000.0
        SCALE_BASE = 512.0

        def _rotate_half(x):
            x = x.reshape(*x.shape[:-1], -1, 2)
            x1, x2 = (x[..., 0], x[..., 1])
            return jnp.stack((-x2, x1), axis=-1).reshape(*x1.shape[:-1], -1)

        def _xpos_rotate(q, k):
            s = q.shape[2]
            t = jnp.arange(s, dtype=jnp.float32)
            inv_freq = 1.0 / THETA ** (jnp.arange(0, DH, 2, dtype=jnp.float32) / DH)
            freqs = t[:, None] * inv_freq[None, :]
            freqs = jnp.repeat(freqs, 2, axis=-1)
            cos, sin = (jnp.cos(freqs), jnp.sin(freqs))
            base = (jnp.arange(0, DH, 2, dtype=jnp.float32) + 0.4 * DH) / (1.4 * DH)
            power = (t - s // 2) / SCALE_BASE
            scale = base[None, :] ** power[:, None]
            scale = jnp.concatenate((scale, scale), axis=-1)
            q = q * cos * scale + _rotate_half(q) * sin * scale
            inv_scale = 1.0 / scale
            k = k * cos * inv_scale + _rotate_half(k) * sin * inv_scale
            return (q, k)
        b, s, _ = x.shape

        def split_heads(t):
            return t.reshape(b, s, NUM_HEADS, DH).transpose(0, 2, 1, 3)
        q_mat = split_heads(x @ Wq.T + bq)
        k_mat = split_heads(x @ Wv.T + bv)
        v_mat = split_heads(x @ Wk.T + bk)
        q_mat, k_mat = _xpos_rotate(q_mat, k_mat)
        scores = jnp.einsum('bhqd,bhkd->bhqk', q_mat, k_mat) / math.sqrt(DH * NUM_HEADS)
        causal = jnp.tril(jnp.ones((s, s), dtype=bool))
        scores = jnp.where(causal[None, None], scores, -jnp.inf)
        weights = jax.nn.softmax(scores, axis=-1)
        inter = jnp.einsum('bhqk,bhkd->bhqd', weights, v_mat)
        inter = inter.transpose(0, 2, 1, 3).reshape(b, s, DIM)
        return inter @ Wo.T + bo

    def _L0_ffn_ref(x, gate_w, wg, wu, wd, sg, su, sd):
        import jax, jax.numpy as jnp
        import numpy as np
        DIM = 256
        INTER = 128
        E = 8
        TOP_K = 2
        ROUTE_SCALE = 1.0
        B, S, D = x.shape
        xf = x.reshape(-1, D)
        N = xf.shape[0]
        scores = jax.nn.softmax(xf @ gate_w.T, axis=-1)
        _, idx = jax.lax.top_k(scores, TOP_K)
        weights = jnp.take_along_axis(scores, idx, axis=-1) * ROUTE_SCALE
        cw = jnp.zeros((N, E), dtype=xf.dtype)
        cw = cw.at[jnp.arange(N)[:, None], idx].add(weights)
        g = jnp.einsum('nd,efd->nef', xf, wg)
        u = jnp.einsum('nd,efd->nef', xf, wu)
        h = jax.nn.silu(g) * u
        y = jnp.einsum('nef,edf->ned', h, wd)
        routed = jnp.einsum('ned,ne->nd', y, cw)
        shared = jax.nn.silu(xf @ sg.T) * (xf @ su.T) @ sd.T
        return (routed + shared).reshape(B, S, D)
    x = L0_attn_x
    x = _layernorm(x + _L0_attn_ref(x, L0_attn_Wq, L0_attn_bq, L0_attn_Wk, L0_attn_bk, L0_attn_Wv, L0_attn_bv, L0_attn_Wo, L0_attn_bo), axis=-1)
    x = _layernorm(x + _L0_ffn_ref(x, L0_ffn_gate_w, L0_ffn_wg, L0_ffn_wu, L0_ffn_wd, L0_ffn_sg, L0_ffn_su, L0_ffn_sd), axis=-1)
    return x

_drawn_inputs = setup_inputs


def setup_inputs(seed=0):
    import zlib

    import numpy as np

    out = dict(_drawn_inputs(seed))
    spreads = {'L0_attn_bq': (0.0, 0.8),
     'L0_attn_bk': (0.0, 0.1),
     'L0_attn_bv': (0.0, 0.8),
     'L0_attn_bo': (0.0, 0.1)}
    factors = {'L0_attn_Wq': 3.464, 'L0_attn_Wv': 3.175}
    for name, (base, spread) in spreads.items():
        noise = np.random.default_rng([zlib.crc32(name.encode()), seed]).standard_normal(out[name].shape)
        drawn = base * np.exp(spread * noise) if base else spread * noise
        out[name] = jnp.asarray(drawn.astype(out[name].dtype))
    for name, factor in factors.items():
        out[name] = (out[name] * factor).astype(out[name].dtype)
    return out
```

```python
from contextlib import ExitStack

import numpy as np

import concourse.bass as bass
from concourse import mybir
from concourse.alu_op_type import AluOpType as ALU

ACT = mybir.ActivationFunctionType
AX = mybir.AxisListType
F32 = mybir.dt.float32
BF16 = mybir.dt.bfloat16
U32 = mybir.dt.uint32

P = 128
BATCH, SEQ, DIM = 2, 2048, 256
HEADS, DH = 16, 16
EXPERTS, INTER = 8, 128
ALL_EXPERTS = EXPERTS + 1
TILES = SEQ // P
BLOCK = 512
BLOCKS = SEQ // BLOCK
TPB = BLOCK // P
CHUNKS = DIM // P
GROUP = 4
GROUPS = HEADS // GROUP
PARTS = 3
QK = 2 * DIM
Q_PARTS = (0, 0, 1, 1, 0, 2)
K_PARTS = (0, 1, 0, 1, 2, 0)
SLOT_ROWS = DH * len(Q_PARTS)
SCORE_ROWS = SLOT_ROWS + PARTS
V_STRIDE = DH + 1
COL_TILE = 32
V_COLS = (HEADS - 1) * V_STRIDE + COL_TILE
BANK = 512
BANKS = 8
SCORE_UNITS = 3
EPS = 1e-5
SOFTMAX_SCALE = 1.0 / (DH * HEADS) ** 0.5
MASKED = -1e30


class Stage:

    def __init__(self, ctx, nc, name, step=1):
        self.sem = ctx.enter_context(nc.semaphore(name))
        self.step = step
        self.count = 0

    def done(self, instruction):
        self.count += self.step
        instruction.then_inc(self.sem, self.step)
        return self.sem, self.count


def wait(engine, *marks):
    for mark in marks:
        if mark is not None:
            engine.wait_ge(*mark)


def build_program(nc, t):
    with ExitStack() as ctx:
        emit(nc, t, ctx)


def emit(nc, t, ctx):
    pe, act, dve, pool, sp = nc.tensor, nc.scalar, nc.vector, nc.gpsimd, nc.sync

    def sbuf(name, shape, dtype=F32):
        return ctx.enter_context(nc.sbuf_tensor(name, shape, dtype))

    def stage(name):
        return Stage(ctx, nc, name)

    def dma_stage(name):
        return Stage(ctx, nc, name, 16)

    w_qkv = sbuf("w_qkv", [P, CHUNKS, 3 * DIM])
    b_qkv = sbuf("b_qkv", [P, 3 * DIM])
    w_out = sbuf("w_out", [P, CHUNKS, DIM])
    b_out = sbuf("b_out", [P, DIM])
    w_router = sbuf("w_router", [P, CHUNKS, EXPERTS])
    w_gate = sbuf("w_gate", [P, CHUNKS, ALL_EXPERTS * INTER])
    w_up = sbuf("w_up", [P, CHUNKS, ALL_EXPERTS * INTER])
    w_down = sbuf("w_down", [P, ALL_EXPERTS, DIM])
    rot_cos = sbuf("rot_cos", [P, TILES, 2, DH])
    rot_sin = sbuf("rot_sin", [P, TILES, 2, DH])
    ident = sbuf("ident", [P, P])
    ident16 = sbuf("ident16", [P, P], BF16)
    causal16 = sbuf("causal16", [P, P], BF16)
    eps = sbuf("eps", [P, 1])
    expert_ids = sbuf("expert_ids", [P, EXPERTS])

    x_tok = sbuf("x_tok", [P, TILES, DIM])
    x_t = sbuf("x_t", [P, CHUNKS, SEQ])
    v_aug = sbuf("v_aug", [P, TILES, V_COLS])
    attn = x_t[:].rearrange("p c n -> p (c n)").rearrange("p (n c) -> p n c", c=DIM)
    q_stacks = sbuf("q_stacks", [P, 2, GROUP, SEQ], BF16)
    q_stack = [q_stacks[:, i, :, :] for i in range(2)]
    k_stack = [sbuf(f"k_stack{i}", [P, GROUP, SEQ], BF16) for i in range(2)]
    shift = sbuf("shift", [P, TILES, HEADS])
    shift16 = sbuf("shift16", [P, TILES, PARTS, HEADS], BF16)
    shift_t = sbuf("shift_t", [PARTS * HEADS, SEQ], BF16)

    probs = [sbuf(f"probs{i}", [P, 2, BLOCK]) for i in range(4)]
    work = sbuf("work", [P, 6144])
    qk_raw = [work[:, i * QK:(i + 1) * QK] for i in range(2)]
    qk_rot = [work[:, (2 + i) * QK:(3 + i) * QK] for i in range(2)]
    qk_swap = [work[:, (4 + i) * QK:(5 + i) * QK] for i in range(2)]
    qk_part = [work[:, 3072 + i * 768:3840 + i * 768].bitcast(BF16)
               .rearrange("p (n c) -> p n c", n=PARTS) for i in range(2)]
    part_t = (q_stacks[:].rearrange("p a h n -> p (a h n)")[:, 0:2 * PARTS * 4 * BLOCK]
              .rearrange("p (a n q) -> p a n q", a=2, q=BLOCK))
    o_t = [work[:, i * BLOCK:(i + 1) * BLOCK] for i in range(2)]
    recip = [sbuf(f"recip{i}", [P, TPB * GROUP]) for i in range(2)]

    psum = ctx.enter_context(nc.psum_tensor("psum", [P, BANKS * BANK], F32))

    def bank(i, n=1):
        return psum[:, i * BANK:(i + n) * BANK]

    weights_in = dma_stage("weights_in")
    for buf, name in ((w_qkv, "w_qkv"), (b_qkv, "b_qkv"), (rot_cos, "rot_cos"), (rot_sin, "rot_sin"),
                      (ident, "ident")):
        proj_in = weights_in.done(sp.dma_start(buf[:], t[name]))
    late_weights_in = dma_stage("late_weights_in")

    const_made = stage("const_made")
    const_made.done(pool.memset(eps[:], EPS))
    zeros_made = const_made.done(pool.memset(causal16[:], 0.0))
    for e in range(EXPERTS):
        const_made.done(pool.memset(expert_ids[:, e:e + 1], float(e)))
    v_ones = const_made.done(pool.memset(v_aug[:], 1.0))
    ones_made = stage("ones_made")
    for i in range(2):
        ones_rows = ones_made.done(dve.memset(k_stack[i][SLOT_ROWS:SLOT_ROWS + PARTS, :, :], 1.0))
    wait(pool, zeros_made)
    consts = const_made.done(pool.affine_select(out=causal16[:], in_=causal16[:], pattern=[[-1, P]],
                                                compare_op=ALU.is_ge, fill=MASKED, base=0,
                                                channel_multiplier=1))
    cast_done = stage("cast_done")
    wait(dve, proj_in)
    ident16_made = cast_done.done(dve.tensor_copy(ident16[:], ident[:]))

    s = {name: stage(name) for name in (
        "pe_qkv", "pe_part_t", "dve_bias", "pool_swap", "dve_rot", "act_part", "dve_part",
        "act_part_t", "pe_max", "dve_max", "dve_shift", "pe_shift_t", "act_shift_t",
        "pe_score", "act_exp", "pool_causal", "pe_attn", "dve_o_t", "pe_o", "dve_norm",
        "pe_attn_t", "act_attn_t", "pe_out", "dve_res", "dve_ln", "act_sqrt", "pe_x1_t",
        "act_x1_t", "pe_router", "dve_router", "act_router", "pe_gate", "pe_up", "act_silu",
        "dve_h", "pe_down", "dve_y", "dve_out")}
    parts_out = [dma_stage(f"parts_out{i}") for i in range(2)]
    shift_out = dma_stage("shift_out")
    x_in = dma_stage("x_in")
    xt_in = [dma_stage(f"xt_in{i}") for i in range(BLOCKS)]
    stack_in = [dma_stage(f"stack_in{i}") for i in range(2)]
    shift_in = [dma_stage(f"shift_in{i}") for i in range(2)]
    y_out = [dma_stage(f"y_out{i}") for i in range(BLOCKS)]

    parts_dram = t["parts_dram"]
    shift_dram = t["shift_dram"]

    last_batch_done = None
    x1_t_read = None

    for b in range(BATCH):
        wait(sp, *(last_batch_done or ()))
        xt_marks = []
        for blk in range(BLOCKS):
            tok = slice(b * SEQ + blk * BLOCK, b * SEQ + (blk + 1) * BLOCK)
            xt_marks.append(xt_in[blk].done(sp.dma_start(
                x_t[:, :, blk * BLOCK:(blk + 1) * BLOCK],
                t["x_t"][:, tok].rearrange("(c p) n -> p c n", p=P))))
        x_loaded = x_in.done(sp.dma_start(
            x_tok[:], t["x"][b * SEQ:(b + 1) * SEQ, :].rearrange("(n p) c -> p n c", p=P)))
        if b == 0:
            for buf, name in ((w_out, "w_out"), (b_out, "b_out"), (w_router, "w_router"),
                              (w_gate, "w_gate"), (w_up, "w_up"), (w_down, "w_down")):
                late = late_weights_in.done(sp.dma_start(buf[:], t[name]))

        qkv_of, bias_of, rot_of, part_of, swap_of, tr_of, evac_of = {}, {}, {}, {}, {}, {}, {}
        parts_written = []
        wait(pe, proj_in, ident16_made)
        wait(dve, v_ones, *(last_batch_done or ()))
        wait(act, *(last_batch_done or ()))
        wait(pool, proj_in)

        def project(i):
            buf = i % 2
            wait(pe, xt_marks[i // TPB])
            wait(pe, bias_of.get(i - 2))
            for c in range(CHUNKS):
                lhs = x_t[:, c, i * P:(i + 1) * P]
                pe.matmul(bank(buf)[:, 0:QK], lhs, w_qkv[:, c, 0:QK],
                          start=(c == 0), stop=(c == CHUNKS - 1))
                mm = pe.matmul(bank(2 + buf)[:, 0:DIM], lhs, w_qkv[:, c, QK:QK + DIM],
                               start=(c == 0), stop=(c == CHUNKS - 1))
            qkv_of[i] = s["pe_qkv"].done(mm)

        def rotate_and_split(i):
            buf = i % 2
            raw, rot, swp, part = qk_raw[buf], qk_rot[buf], qk_swap[buf], qk_part[buf]
            wait(dve, qkv_of[i], rot_of.get(i - 2), swap_of.get(i - 2))
            raw_made = s["dve_bias"].done(dve.tensor_tensor(raw, bank(buf)[:, 0:QK], b_qkv[:, 0:QK], ALU.add))
            bias_of[i] = s["dve_bias"].done(dve.tensor_tensor(
                v_aug[:, i, 0:HEADS * V_STRIDE].rearrange("p (h d) -> p h d", h=HEADS)[:, :, 0:DH],
                bank(2 + buf)[:, 0:DIM].rearrange("p (h d) -> p h d", h=HEADS),
                b_qkv[:, QK:QK + DIM].rearrange("p (h d) -> p h d", h=HEADS), ALU.add))
            wait(pool, raw_made, rot_of.get(i - 2))
            pair = "p (a h f e) -> p a h f e"
            raw5 = raw.rearrange(pair, a=2, h=HEADS, e=2)
            swp5 = swp.rearrange(pair, a=2, h=HEADS, e=2)
            sin5 = rot_sin[:, i, :, :].rearrange("p a (f e) -> p a f e", e=2)
            for e in range(2):
                for a in range(2):
                    op = pool.tensor_tensor(
                        swp5[:, a, :, :, e], raw5[:, a, :, :, 1 - e],
                        sin5[:, a, :, e].unsqueeze(1).to_broadcast([P, HEADS, DH // 2]), ALU.mult)
            swap_of[i] = s["pool_swap"].done(op)
            wait(dve, raw_made, evac_of.get(i - 2), part_of.get(i - 2))
            cos4 = rot_cos[:, i, :, :].unsqueeze(2).to_broadcast([P, 2, HEADS, DH])
            cos_done = s["dve_rot"].done(dve.tensor_tensor(
                rot.rearrange("p (a h d) -> p a h d", a=2, h=HEADS),
                raw.rearrange("p (a h d) -> p a h d", a=2, h=HEADS), cos4, ALU.mult))
            wait(dve, swap_of[i], cos_done)
            rot_of[i] = s["dve_rot"].done(dve.tensor_tensor(rot, rot, swp, ALU.add))
            for n in range(PARTS):
                if n == 0:
                    wait(act, rot_of[i], tr_of.get(i - 2))
                else:
                    wait(act, left)
                cast = s["act_part"].done(act.copy(part[:, n, :], rot))
                if n < PARTS - 1:
                    wait(dve, cast)
                    left = s["dve_part"].done(dve.tensor_tensor(rot, rot, part[:, n, :], ALU.subtract))
            part_of[i] = cast

        def transpose_parts(i):
            buf = i % 2
            part = qk_part[buf]
            blk, at = divmod(i, TPB)
            wait(pe, part_of[i], evac_of.get(i - 2))
            tb = bank(4 + 2 * buf, 2).bitcast(BF16)
            for n in range(PARTS * 4):
                tr = pe.transpose(tb[:, n * P:(n + 1) * P], part[:, n // 4, (n % 4) * P:(n % 4 + 1) * P],
                                  ident16[:])
            tr_of[i] = s["pe_part_t"].done(tr)
            wait(act, tr_of[i])
            if at == 0 and blk >= 2:
                wait(act, parts_written[blk - 2])
            evac_of[i] = s["act_part_t"].done(act.copy(
                part_t[:, blk % 2, :, at * P:(at + 1) * P],
                tb[:, 0:PARTS * 4 * P].rearrange("p (n q) -> p n q", q=P)))
            if at == TPB - 1:
                wait(sp, evac_of[i])
                tok = slice(b * SEQ + blk * BLOCK, b * SEQ + (blk + 1) * BLOCK)
                parts_written.append(parts_out[blk % 2].done(sp.dma_start(
                    parts_dram[:, :, tok].rearrange("n p q -> p n q"), part_t[:, blk % 2, :, :])))

        for i in range(TILES + 2):
            if i < TILES:
                project(i)
            if 1 <= i <= TILES:
                rotate_and_split(i - 1)
            if i >= 2:
                transpose_parts(i - 2)
        projected = (evac_of[TILES - 1], bias_of[TILES - 1])

        stack_free = {}

        def load_stack(n, with_shift):
            g, half = n % GROUPS, n % 2
            wait(sp, *parts_written[-2:], *stack_free.get(n - 2, ()))
            tok = slice(b * SEQ, (b + 1) * SEQ)
            for dst, which, order in ((q_stack[half], 0, Q_PARTS), (k_stack[half], 1, K_PARTS)):
                for slot, part in enumerate(order):
                    row0 = g * GROUP * DH
                    chunk = part * 4 + which * CHUNKS + row0 // P
                    src = parts_dram[chunk, row0 % P:row0 % P + GROUP * DH, tok]
                    mark = stack_in[half].done(sp.dma_start(
                        dst[slot * DH:(slot + 1) * DH, :, :],
                        src.rearrange("(h d) n -> d h n", d=DH)))
            marks = [mark]
            if with_shift:
                wait(sp, shift_written)
                marks.append(shift_in[half].done(sp.dma_start(
                    q_stack[half][SLOT_ROWS:SLOT_ROWS + PARTS, :, :],
                    shift_dram[:, g * GROUP:(g + 1) * GROUP, tok])))
            return marks

        stacks = {0: load_stack(0, False)}
        max_of = []
        wait(pe, consts, ones_rows, *projected)
        wait(dve, *projected)
        for g in range(GROUPS):
            if g + 1 < GROUPS:
                stacks[g + 1] = load_stack(g + 1, False)
            qs, ks = q_stack[g % 2], k_stack[g % 2]
            wait(pe, *stacks[g])
            for j in range(GROUP):
                for i in range(TILES):
                    n = len(max_of)
                    if n >= 2:
                        wait(pe, max_of[n - 2])
                    base = (n % 2) * 4
                    keys = (i + 1) * P
                    pe.matmul(bank(base + i // TPB)[:, i % TPB * P:(i % TPB + 1) * P], ident16[:],
                              causal16[:], start=True, stop=False, skip_group_check=True)
                    for k0 in range(0, keys, BLOCK):
                        width = min(BLOCK, keys - k0)
                        mm = pe.matmul(bank(base + k0 // BLOCK)[:, 0:width],
                                       qs[0:SLOT_ROWS, j, i * P:(i + 1) * P],
                                       ks[0:SLOT_ROWS, j, k0:k0 + width],
                                       start=k0 + width < keys, stop=True, skip_group_check=True)
                    wait(dve, s["pe_max"].done(mm))
                    max_of.append(s["dve_max"].done(dve.tensor_reduce(
                        shift[:, i, g * GROUP + j:g * GROUP + j + 1], bank(base, 4)[:, 0:keys],
                        AX.X, ALU.max, negate=True)))
            stack_free[g] = (max_of[-1],)

        wait(dve, max_of[-1])
        for n in range(PARTS):
            cast = s["dve_shift"].done(dve.tensor_copy(shift16[:, :, n, :], shift[:]))
            wait(dve, cast)
            if n < PARTS - 1:
                wait(dve, s["dve_shift"].done(dve.tensor_tensor(
                    shift[:], shift[:], shift16[:, :, n, :], ALU.subtract)))
        wait(pe, cast)
        tb = bank(0, 2).bitcast(BF16)
        for i in range(TILES):
            tr = pe.transpose(tb[0:PARTS * HEADS, i * P:(i + 1) * P], shift16[:, i, :, :], ident16[:])
        wait(act, s["pe_shift_t"].done(tr))
        shift_rows = s["act_shift_t"].done(act.copy(shift_t[:], tb[0:PARTS * HEADS, :]))
        wait(sp, shift_rows)
        shift_written = shift_out.done(sp.dma_start(
            shift_dram[:, :, b * SEQ:(b + 1) * SEQ].rearrange("a h n -> (a h) n"), shift_t[:]))

        unit = 0
        exp_of, probs_read, norm_of = {}, {}, {}
        pending = None

        def attend(step):
            units, kt, off, qb, g, out_n, first, last = step
            o_bank = bank(6 + out_n % 2)
            for u in units:
                wait(pe, *exp_of[u])
            if first:
                wait(pe, norm_of.get(out_n - 2))
            for j in range(GROUP):
                h = g * GROUP + j
                mm = pe.matmul(o_bank[j * COL_TILE:(j + 1) * COL_TILE, off:BLOCK],
                               v_aug[:, kt, h * V_STRIDE:h * V_STRIDE + COL_TILE],
                               probs[units[j // 2] % 4][:, j % 2, off:BLOCK],
                               start=first, stop=last, skip_group_check=True)
            mark = s["pe_attn"].done(mm)
            for u in units:
                probs_read[u] = mark
            if last:
                finish_output(mark, qb, g, out_n)
            return mark

        def finish_output(mark, qb, g, out_n):
            o_bank, ot, rc = bank(6 + out_n % 2), o_t[out_n % 2], recip[out_n % 2]
            wait(dve, mark)
            copied = s["dve_o_t"].done(dve.tensor_copy(ot, o_bank))
            wait(pe, copied)
            for a in range(TPB):
                tr = pe.transpose(o_bank[:, a * P:(a + 1) * P], ot[:, a * P:(a + 1) * P], ident[:])
            turned = s["pe_o"].done(tr)
            wait(dve, turned)
            heads = o_bank.rearrange("p (n d) -> p n d", d=COL_TILE)
            inverted = s["dve_norm"].done(dve.reciprocal(rc[:], heads[:, :, DH]))
            wait(dve, inverted)
            norm_of[out_n] = s["dve_norm"].done(dve.tensor_tensor(
                attn[:, qb * TPB:(qb + 1) * TPB, g * GROUP * DH:(g + 1) * GROUP * DH]
                .rearrange("p n (h d) -> p n h d", d=DH),
                heads[:, :, 0:DH].rearrange("p (n h) d -> p n h d", n=TPB),
                rc[:].rearrange("p (n h) -> p n h", n=TPB).unsqueeze(3).to_broadcast([P, TPB, GROUP, DH]),
                ALU.mult))

        n0 = GROUPS
        stacks[n0] = load_stack(n0, True)
        wait(pe, shift_rows)
        out_n = 0
        for g in range(GROUPS):
            if g + 1 < GROUPS:
                stacks[n0 + g + 1] = load_stack(n0 + g + 1, True)
            qs, ks = q_stack[g % 2], k_stack[g % 2]
            wait(pe, *stacks[n0 + g])
            for qb in range(BLOCKS):
                key_tiles = (qb + 1) * TPB
                for kt in reversed(range(key_tiles)):
                    off = max(0, kt * P - qb * BLOCK)
                    units = []
                    for pair in range(2):
                        u = unit
                        unit += 1
                        units.append(u)
                        s_unit = bank(2 * (u % SCORE_UNITS), 2).rearrange("p (h q) -> p h q", h=2)
                        if u >= SCORE_UNITS:
                            wait(pe, exp_of[u - SCORE_UNITS][0])
                        for e in range(2):
                            j = pair * 2 + e
                            mm = pe.matmul(s_unit[:, e, off:BLOCK],
                                           ks[0:SCORE_ROWS, j, kt * P:(kt + 1) * P],
                                           qs[0:SCORE_ROWS, j, qb * BLOCK + off:(qb + 1) * BLOCK],
                                           start=True, stop=True)
                        scored = s["pe_score"].done(mm)
                        pr = probs[u % 4]
                        wait(act, scored, probs_read.get(u - 4))
                        exp_done = s["act_exp"].done(act.activation(
                            pr[:, :, off:BLOCK], s_unit[:, :, off:BLOCK], ACT.Exp, scale=SOFTMAX_SCALE))
                        marks = [exp_done]
                        if kt >= qb * TPB:
                            wait(pool, exp_done)
                            marks.append(s["pool_causal"].done(pool.affine_select(
                                out=pr[:, :, off:off + P], in_=pr[:, :, off:off + P],
                                pattern=[[0, 2], [1, P]], compare_op=ALU.is_ge, fill=0.0, base=0,
                                channel_multiplier=-1)))
                        exp_of[u] = tuple(marks)
                    if pending is not None:
                        attended = attend(pending)
                    pending = (units, kt, off, qb, g, out_n, kt == key_tiles - 1, kt == 0)
                out_n += 1
            stack_free[n0 + g] = (scored,)
        attend(pending)
        attention_done = norm_of[out_n - 1]

        attn_t = work[:, 0:2 * CHUNKS * P].rearrange("p (a c q) -> p a c q", a=2, c=CHUNKS)
        stats = work[:, 2048:2048 + TILES * 6].rearrange("p (n k) -> p n k", k=6)
        mean_var = work[:, 2176:2176 + TILES * 2].rearrange("p (n k) -> p n k", k=2)
        rstd = work[:, 2240:2240 + TILES]
        wait(pool, x_loaded, late)
        for i in range(TILES):
            with_bias = s["pool_swap"].done(pool.tensor_tensor(x_tok[:, i, :], x_tok[:, i, :], b_out[:], ALU.add))
        wait(pe, attention_done, late)
        wait(act, attention_done)
        res_of, at_of = {}, {}
        for i in range(TILES):
            buf = i % 2
            wait(pe, at_of.get(i - 2))
            for c in range(CHUNKS):
                tr = pe.transpose(bank(buf)[:, c * P:(c + 1) * P], attn[:, i, c * P:(c + 1) * P], ident[:])
            wait(act, s["pe_attn_t"].done(tr))
            at_of[i] = s["act_attn_t"].done(act.copy(
                attn_t[:, buf, :, :], bank(buf)[:, 0:DIM].rearrange("p (c q) -> p c q", c=CHUNKS)))
            wait(pe, at_of[i], res_of.get(i - 2))
            for c in range(CHUNKS):
                mm = pe.matmul(bank(2 + buf)[:, 0:DIM], attn_t[:, buf, c, :], w_out[:, c, :],
                               start=(c == 0), stop=(c == CHUNKS - 1))
            wait(dve, s["pe_out"].done(mm), with_bias)
            res_of[i] = s["dve_res"].done(dve.tensor_tensor(
                x_tok[:, i, :], bank(2 + buf)[:, 0:DIM], x_tok[:, i, :], ALU.add))

        def normalise(wanted, tag, out=None):
            wait(dve, *wanted)
            for i in range(TILES):
                m = s["dve_ln"].done(dve.bn_stats(stats[:, i, :], x_tok[:, i, :]))
            wait(dve, m)
            for i in range(TILES):
                m = s["dve_ln"].done(dve.bn_aggr(mean_var[:, i, :], stats[:, i, :]))
            wait(act, m)
            root = s["act_sqrt"].done(act.activation(rstd, mean_var[:, :, 1], ACT.Sqrt, bias=eps[:]))
            wait(dve, root)
            m = s["dve_ln"].done(dve.reciprocal(rstd, rstd))
            wait(dve, m)
            marks = []
            for i in range(TILES):
                marks.append(s["dve_ln"].done(dve.tensor_scalar(
                    x_tok[:, i, :], x_tok[:, i, :], mean_var[:, i, 0:1], rstd[:, i:i + 1],
                    ALU.subtract, ALU.mult)))
            return marks

        ln1 = normalise([res_of[TILES - 1], consts], "ln1")

        xt_of = {}
        for i in range(TILES):
            wait(pe, ln1[i], xt_of.get(i - 2))
            buf = i % 2
            for c in range(CHUNKS):
                tr = pe.transpose(bank(buf)[:, c * P:(c + 1) * P], x_tok[:, i, c * P:(c + 1) * P], ident[:])
            wait(act, s["pe_x1_t"].done(tr))
            xt_of[i] = s["act_x1_t"].done(act.copy(
                x_t[:, :, i * P:(i + 1) * P], bank(buf)[:, 0:DIM].rearrange("p (c q) -> p c q", c=CHUNKS)))
        logits = bank(2)[:, 0:TILES * EXPERTS].rearrange("p (n e) -> p n e", e=EXPERTS)
        for i in range(TILES):
            wait(pe, xt_of[i])
            for c in range(CHUNKS):
                mm = pe.matmul(logits[:, i, :], x_t[:, c, i * P:(i + 1) * P], w_router[:, c, :],
                               start=(c == 0), stop=(c == CHUNKS - 1))
        NE = TILES * EXPERTS
        router = work[:, 2304:2304 + 8 * NE]

        def room(k, n=NE):
            return router[:, k * NE:k * NE + n]

        score = room(0).rearrange("p (n e) -> p n e", e=EXPERTS)
        top = room(1).rearrange("p (n e) -> p n e", e=EXPERTS)
        top_at = room(2).bitcast(U32).rearrange("p (n e) -> p n e", e=EXPERTS)
        top_atf = room(3).rearrange("p (n e) -> p n e", e=EXPERTS)
        pick = room(4).rearrange("p (n e) -> p n e", e=EXPERTS)
        pick2 = room(5).rearrange("p (n e) -> p n e", e=EXPERTS)
        combine = room(6).rearrange("p (n e) -> p n e", e=EXPERTS)
        row_stat = room(7, TILES)
        r = s["dve_router"]

        def over_experts(ap):
            return ap.unsqueeze(2).to_broadcast([P, TILES, EXPERTS])

        wait(dve, s["pe_router"].done(mm))
        m = r.done(dve.tensor_reduce(row_stat, logits, AX.X, ALU.max))
        wait(dve, m)
        m = r.done(dve.tensor_tensor(score, logits, over_experts(row_stat), ALU.subtract))
        wait(act, m)
        m = s["act_router"].done(act.activation(score, score, ACT.Exp))
        wait(dve, m)
        m = r.done(dve.tensor_reduce(row_stat, score, AX.X, ALU.add))
        wait(dve, m)
        m = r.done(dve.reciprocal(row_stat, row_stat))
        wait(dve, m)
        m = r.done(dve.tensor_tensor(score, score, over_experts(row_stat), ALU.mult))
        wait(dve, m)
        for i in range(TILES):
            m = r.done(dve.max(top[:, i, :], score[:, i, :]))
        wait(dve, m)
        for i in range(TILES):
            m = r.done(dve.max_index(top_at[:, i, :], top[:, i, :], score[:, i, :]))
        wait(dve, m)
        m = r.done(dve.tensor_copy(top_atf, top_at))
        wait(dve, m)
        ids = expert_ids[:].unsqueeze(1).to_broadcast([P, TILES, EXPERTS])
        for k, dst in ((0, pick), (1, pick2)):
            m = r.done(dve.tensor_tensor(dst, ids, over_experts(top_atf[:, :, k]), ALU.is_equal))
        wait(dve, m)
        m = r.done(dve.tensor_tensor(pick, pick, pick2, ALU.add))
        wait(dve, m)
        combined = r.done(dve.tensor_tensor(combine, pick, score, ALU.mult))

        silu = [work[:, 0:512], work[:, 512:1024]]
        hidden = [work[:, 1024:1536], work[:, 1536:2048]]
        jobs = [(blk, e) for blk in range(BLOCKS) for e in range(ALL_EXPERTS)]
        up_of, silu_of, h_of, down_of, y_of = {}, {}, {}, {}, {}
        wait(pe, combined, late)
        wait(dve, combined, late)

        def gate_up(n):
            blk, e = jobs[n]
            buf = n % 2
            wait(pe, h_of.get(n - 2))
            for dst, w, st in ((bank(buf), w_gate, "pe_gate"), (bank(2 + buf), w_up, "pe_up")):
                for c in range(CHUNKS):
                    mm = pe.matmul(dst, w[:, c, e * INTER:(e + 1) * INTER],
                                   x_t[:, c, blk * BLOCK:(blk + 1) * BLOCK],
                                   start=(c == 0), stop=(c == CHUNKS - 1))
                mark = s[st].done(mm)
                if st == "pe_gate":
                    wait(act, mark, h_of.get(n - 2))
                    silu_of[n] = s["act_silu"].done(act.activation(silu[buf], bank(buf), ACT.Silu))
            wait(dve, mark, silu_of[n], down_of.get(n - 2))
            h_of[n] = s["dve_h"].done(dve.tensor_tensor(hidden[buf], bank(2 + buf), silu[buf], ALU.mult))

        def down(n):
            blk, e = jobs[n]
            buf = n % 2
            wait(pe, h_of[n])
            for a in range(TPB):
                i = blk * TPB + a
                wait(pe, y_of.get((n - 1, a)))
                mm = pe.matmul(bank(4 + a)[:, 0:DIM], hidden[buf][:, a * P:(a + 1) * P], w_down[:, e, :],
                               start=True, stop=True)
                down_of[n] = s["pe_down"].done(mm)
                wait(dve, down_of[n], y_of.get((n - 1, a)))
                if e == 0:
                    op = dve.tensor_tensor(x_tok[:, i, :], bank(4 + a)[:, 0:DIM], x_tok[:, i, :], ALU.add)
                else:
                    op = dve.scalar_tensor_tensor(
                        out=x_tok[:, i, :], in0=bank(4 + a)[:, 0:DIM], scalar=combine[:, i, e - 1:e],
                        in1=x_tok[:, i, :], op0=ALU.mult, op1=ALU.add)
                y_of[(n, a)] = s["dve_y"].done(op)

        for n in range(len(jobs) + 1):
            if n < len(jobs):
                gate_up(n)
            if n >= 1:
                down(n - 1)

        ln2 = normalise([y_of[(len(jobs) - 1, TPB - 1)]], "ln2")
        stores = []
        for blk in range(BLOCKS):
            wait(sp, ln2[(blk + 1) * TPB - 1])
            rows = slice(b * SEQ + blk * BLOCK, b * SEQ + (blk + 1) * BLOCK)
            stores.append(y_out[blk].done(sp.dma_start(
                t["out"][rows, :].rearrange("(n p) c -> p n c", p=P),
                x_tok[:, blk * TPB:(blk + 1) * TPB, :])))
        last_batch_done = (ln2[-1], *stores, down_of[len(jobs) - 1])
        for m in last_batch_done:
            wait(pe, m)
            wait(pool, m)

    wait(sp, *last_batch_done)


def rotation_tables():
    f = np.float32
    pos = np.arange(SEQ, dtype=f)
    inv_freq = (f(1.0) / f(10000.0) ** (np.arange(0, DH, 2, dtype=f) / f(DH))).astype(f)
    freqs = np.repeat(pos[:, None] * inv_freq[None, :], 2, axis=-1)
    cos, sin = np.cos(freqs), np.sin(freqs)
    base = (np.arange(0, DH, 2, dtype=f) + f(0.4 * DH)) / f(1.4 * DH)
    power = (pos - f(SEQ // 2)) / f(512.0)
    scale = base[None, :] ** power[:, None]
    scale = np.concatenate((scale, scale), axis=-1).astype(f)
    sign = np.where(np.arange(DH) % 2 == 0, f(-1.0), f(1.0))[None, :]
    both = np.stack((scale, f(1.0) / scale), axis=1)
    cos_t, sin_t = cos[:, None, :] * both, (sin * sign)[:, None, :] * both

    def tiled(a):
        return np.ascontiguousarray(a.reshape(TILES, P, 2, DH).transpose(1, 0, 2, 3).astype(f))

    return tiled(cos_t), tiled(sin_t)


def kernel(L0_attn_x, L0_attn_Wq, L0_attn_bq, L0_attn_Wk, L0_attn_bk, L0_attn_Wv, L0_attn_bv,
           L0_attn_Wo, L0_attn_bo, L0_ffn_gate_w, L0_ffn_wg, L0_ffn_wu, L0_ffn_wd, L0_ffn_sg,
           L0_ffn_su, L0_ffn_sd):
    import concourse.bacc as bacc
    from concourse.bass_utils import run_bass_kernel_spmd

    def chunked(w):
        return w.reshape(-1, P, w.shape[-1]).transpose(1, 0, 2)

    def rows(v):
        return np.broadcast_to(v[None, :], (P, v.shape[0]))

    x = np.asarray(L0_attn_x).reshape(BATCH * SEQ, DIM)
    w_qkv = np.concatenate([np.asarray(w).T for w in (L0_attn_Wq, L0_attn_Wv, L0_attn_Wk)], axis=1)
    b_qkv = np.concatenate([np.asarray(v) for v in (L0_attn_bq, L0_attn_bv, L0_attn_bk)])
    gate = np.concatenate([np.asarray(L0_ffn_sg)[None], np.asarray(L0_ffn_wg)]).reshape(-1, DIM).T
    up = np.concatenate([np.asarray(L0_ffn_su)[None], np.asarray(L0_ffn_wu)]).reshape(-1, DIM).T
    down = np.concatenate([np.asarray(L0_ffn_sd)[None], np.asarray(L0_ffn_wd)]).transpose(2, 0, 1)
    cos_t, sin_t = rotation_tables()
    arrays = {
        "x": x, "x_t": x.T, "w_qkv": chunked(w_qkv), "b_qkv": rows(b_qkv),
        "rot_cos": cos_t, "rot_sin": sin_t, "ident": np.eye(P, dtype=np.float32),
        "w_out": chunked(np.asarray(L0_attn_Wo).T), "b_out": rows(np.asarray(L0_attn_bo)),
        "w_router": chunked(np.asarray(L0_ffn_gate_w).T), "w_gate": chunked(gate),
        "w_up": chunked(up), "w_down": down,
    }
    arrays = {k: np.ascontiguousarray(v) for k, v in arrays.items()}
    nc = bacc.Bacc("TRN2", target_bir_lowering=False, num_devices=1)
    tensors = {k: nc.dram_tensor(k + "_dram", v.shape, mybir.dt.from_np(v.dtype), kind="ExternalInput").ap()
               for k, v in arrays.items()}
    tensors["parts_dram"] = nc.dram_tensor("parts_scratch", (PARTS * 4, P, BATCH * SEQ), BF16, kind="Internal").ap()
    tensors["shift_dram"] = nc.dram_tensor("shift_scratch", (PARTS, HEADS, BATCH * SEQ), BF16, kind="Internal").ap()
    tensors["out"] = nc.dram_tensor("out_dram", (BATCH * SEQ, DIM), F32, kind="ExternalOutput").ap()
    build_program(nc, tensors)
    result = run_bass_kernel_spmd(nc, [{k + "_dram": v for k, v in arrays.items()}], core_ids=[0])
    return result.results[0]["out_dram"].reshape(BATCH, SEQ, DIM)
```

```python
from contextlib import ExitStack
from itertools import chain

import numpy as np

import concourse.bass as bass
from concourse import mybir
from concourse.alu_op_type import AluOpType as ALU

ACT = mybir.ActivationFunctionType
AX = mybir.AxisListType
F32 = mybir.dt.float32
BF16 = mybir.dt.bfloat16
U32 = mybir.dt.uint32
F32R = mybir.dt.float32r

P = 128
BATCH, SEQ, DIM = 2, 2048, 256
HEADS, DH = 16, 16
EXPERTS, INTER = 8, 128
ALL_EXPERTS = EXPERTS + 1
TILES = SEQ // P
BLOCK = 512
BLOCKS = SEQ // BLOCK
TPB = BLOCK // P
CHUNKS = DIM // P
GROUP = 4
GROUPS = HEADS // GROUP
PARTS = 3
QK = 2 * DIM
Q_PARTS = (0, 0, 1, 1, 0, 2)
K_PARTS = (0, 1, 0, 1, 2, 0)
SLOT_ROWS = DH * len(Q_PARTS)
SCORE_ROWS = SLOT_ROWS + PARTS
V_STRIDE = DH + 1
COL_TILE = 32
V_COLS = (HEADS - 1) * V_STRIDE + COL_TILE
ALL_TILES = BATCH * TILES
ALL_BLOCKS = BATCH * BLOCKS
ALL_GROUPS = BATCH * GROUPS
BANK = 512
BANKS = 8
SCORE_BANKS = 3
MAX_KEYS = 2 * BANK
EPS = 1e-5
SOFTMAX_SCALE = 1.0 / (DH * HEADS) ** 0.5
MASKED = -1e30
PROJ_AHEAD = 6
MAX_FROM, MAX_TO = 6, 37


class Stage:

    def __init__(self, ctx, nc, name, step=1):
        self.sem = ctx.enter_context(nc.semaphore(name))
        self.step = step
        self.count = 0

    def done(self, instruction):
        self.count += self.step
        instruction.then_inc(self.sem, self.step)
        return self.sem, self.count


def wait(engine, *marks):
    for mark in marks:
        if mark is not None:
            engine.wait_ge(*mark)


def build_program(nc, t):
    with ExitStack() as ctx:
        e = Emitter(nc, t, ctx)
        with ExitStack() as room:
            emit_attention(e, room)
        with ExitStack() as room:
            emit_feed_forward(e, room)


class Emitter:

    def __init__(self, nc, t, ctx):
        self.nc, self.t, self.ctx = nc, t, ctx
        self.stages = {}
        self.psum = ctx.enter_context(nc.psum_tensor("psum", [P, BANKS * BANK], F32))
        self.ident = self.sbuf("ident", [P, P])
        self.ident16 = self.sbuf("ident16", [P, P], BF16)
        self.tokens = self.sbuf("tokens", [P, ALL_TILES, DIM])
        self.b_out = self.sbuf("b_out", [P, DIM])
        self.eps = self.sbuf("eps", [P, 1])
        self.expert_ids = self.sbuf("expert_ids", [P, EXPERTS])

    def sbuf(self, name, shape, dtype=F32, room=None):
        return (room or self.ctx).enter_context(self.nc.sbuf_tensor(name, shape, dtype))

    def bank(self, i, n=1):
        return self.psum[:, i * BANK:(i + n) * BANK]

    def stage(self, name):
        if name not in self.stages:
            self.stages[name] = Stage(self.ctx, self.nc, name)
        return self.stages[name]

    def dma_stage(self, name):
        if name not in self.stages:
            self.stages[name] = Stage(self.ctx, self.nc, name, 16)
        return self.stages[name]


def advance(work, steps=1):
    for _ in range(steps):
        if next(work, StopIteration) is StopIteration:
            return False
    return True


def emit_attention(e, room):
    nc, t, bank, stage = e.nc, e.t, e.bank, e.stage
    pe, act, dve, pool, sp = nc.tensor, nc.scalar, nc.vector, nc.gpsimd, nc.sync

    def sbuf(name, shape, dtype=F32):
        return e.sbuf(name, shape, dtype, room)

    w_qkv = sbuf("w_qkv", [P, CHUNKS, 3 * DIM])
    b_qkv = sbuf("b_qkv", [P, 3 * DIM])
    rot_cos = sbuf("rot_cos", [P, TILES, 2, DH])
    rot_sin = sbuf("rot_sin", [P, TILES, 2, DH])
    causal16 = sbuf("causal16", [P, P], BF16)
    x_t = [sbuf(f"x_t{i}", [P, CHUNKS, BLOCK]) for i in range(2)]
    v_aug = sbuf("v_aug", [P, ALL_TILES, V_COLS])
    q_stack = [sbuf(f"q_stack{i}", [P, GROUP, SEQ], BF16) for i in range(2)]
    k_stack = [sbuf(f"k_stack{i}", [P, GROUP, SEQ], BF16) for i in range(2)]
    part_t = [half[:].rearrange("p h n -> p (h n)")[:, 0:PARTS * 4 * BLOCK]
              .rearrange("p (n q) -> p n q", q=BLOCK) for half in (q_stack[1], k_stack[1])]
    probs = [sbuf(f"probs{i}", [P, BLOCK]) for i in range(2 * GROUP)]
    row_max = [sbuf(f"row_max{i}", [P, TILES, GROUP, 2]) for i in range(2)]
    shift = sbuf("shift", [P, TILES, GROUP])
    shift16 = sbuf("shift16", [P, TILES, PARTS, GROUP], BF16)
    recip = [sbuf(f"recip{i}", [P, TPB * GROUP]) for i in range(2)]
    work = sbuf("work", [P, 5888])
    qk_raw = [work[:, i * QK:(i + 1) * QK] for i in range(2)]
    qk_swap = [work[:, (2 + i) * QK:(3 + i) * QK] for i in range(2)]
    qk_rot = [work[:, (4 + i) * QK:(5 + i) * QK] for i in range(3)]
    qk_part = [work[:, 7 * QK + i * 768:7 * QK + (i + 1) * 768].bitcast(BF16)
               .rearrange("p (n c) -> p n c", n=PARTS) for i in range(3)]
    o_t = [work[:, i * BLOCK:(i + 1) * BLOCK] for i in range(2)]
    shift_t = work[0:PARTS * GROUP, 2 * BLOCK:2 * BLOCK + SEQ // 2].bitcast(BF16)

    proj_in = None
    xt_in = [e.dma_stage(f"xt_in{i}") for i in range(2)]
    weights_in = e.dma_stage("weights_in")

    def load_x_t(blk):
        return xt_in[blk % 2].done(sp.dma_start(
            x_t[blk % 2][:], t["x_t"][:, blk * BLOCK:(blk + 1) * BLOCK].rearrange("(c p) n -> p c n", p=P)))

    xt_marks = {}
    weights_in.done(sp.dma_start(w_qkv[:], t["w_qkv"]))
    xt_marks[0] = load_x_t(0)
    for buf, name in ((b_qkv, "b_qkv"), (e.ident, "ident"), (rot_cos, "rot_cos"), (rot_sin, "rot_sin")):
        proj_in = weights_in.done(act.dma_start(buf[:], t[name]))
    xt_marks[1] = load_x_t(1)

    const_made = stage("const_made")
    zeros_made = const_made.done(pool.memset(causal16[:], 0.0))
    v_ones = const_made.done(pool.memset(v_aug[:], 1.0))
    const_made.done(pool.memset(e.eps[:], EPS))
    for k in range(EXPERTS):
        const_made.done(pool.memset(e.expert_ids[:, k:k + 1], float(k)))
    wait(pool, zeros_made)
    e.consts = const_made.done(pool.affine_select(
        out=causal16[:], in_=causal16[:], pattern=[[-1, P]], compare_op=ALU.is_ge, fill=MASKED,
        base=0, channel_multiplier=1))
    wait(dve, proj_in)
    e.ident_made = stage("ident_cast").done(dve.tensor_copy(e.ident16[:], e.ident[:]))
    ones_made = stage("ones_made")
    ones_made.done(dve.memset(k_stack[0][SLOT_ROWS:SLOT_ROWS + PARTS, :, :], 1.0))

    parts_out = [e.dma_stage(f"parts_out{i}") for i in range(2)]
    parts_dram = t["parts_dram"]
    qkv_of, bias_of, swap_of, rot_of, cast0_of, cast1_of, part_of, tr_of, evac_of = ({} for _ in range(9))
    left0_of = {}
    parts_written = []

    def project(i):
        blk, at = divmod(i, TPB)
        if at == 0 and blk not in xt_marks:
            wait(sp, qkv_of[(blk - 1) * TPB - 1])
            xt_marks[blk] = load_x_t(blk)
        wait(pe, xt_marks[blk], bias_of.get(i - 1))
        for c in range(CHUNKS):
            lhs = x_t[blk % 2][:, c, at * P:(at + 1) * P]
            pe.matmul(bank(0)[:, 0:QK], lhs, w_qkv[:, c, 0:QK], start=(c == 0), stop=(c == CHUNKS - 1))
            mm = pe.matmul(bank(1)[:, 0:DIM], lhs, w_qkv[:, c, QK:QK + DIM],
                           start=(c == 0), stop=(c == CHUNKS - 1))
        qkv_of[i] = stage("pe_qkv").done(mm)

    def add_bias(i):
        raw, swp, rot = qk_raw[i % 2], qk_swap[i % 2], qk_rot[i % 3]
        wait(dve, qkv_of[i], swap_of.get(i - 2))
        raw_made = stage("dve_bias").done(dve.tensor_tensor(raw, bank(0)[:, 0:QK], b_qkv[:, 0:QK], ALU.add))
        bias_of[i] = stage("dve_bias").done(dve.tensor_tensor(
            v_aug[:, i, 0:HEADS * V_STRIDE].rearrange("p (h d) -> p h d", h=HEADS)[:, :, 0:DH],
            bank(1)[:, 0:DIM].rearrange("p (h d) -> p h d", h=HEADS),
            b_qkv[:, QK:QK + DIM].rearrange("p (h d) -> p h d", h=HEADS), ALU.add))
        wait(pool, raw_made, rot_of.get(i - 2), part_of.get(i - 3))
        pool.tensor_tensor(
            rot.rearrange("p (a h d) -> p a h d", a=2, h=HEADS),
            raw.rearrange("p (a h d) -> p a h d", a=2, h=HEADS),
            rot_cos[:, i % TILES, :, :].unsqueeze(2).to_broadcast([P, 2, HEADS, DH]), ALU.mult)
        pair = "p (a h f e) -> p a h f e"
        raw5 = raw.rearrange(pair, a=2, h=HEADS, e=2)
        swp5 = swp.rearrange(pair, a=2, h=HEADS, e=2)
        sin4 = rot_sin[:, i % TILES, :, :].rearrange("p a (f e) -> p a f e", e=2)
        for k in range(2):
            op = pool.tensor_tensor(
                swp5[:, :, :, :, k], raw5[:, :, :, :, 1 - k],
                sin4[:, :, :, k].unsqueeze(2).to_broadcast([P, 2, HEADS, DH // 2]), ALU.mult)
        swap_of[i] = stage("pool_rot").done(op)

    def rotate(i):
        rot, part = qk_rot[i % 3], qk_part[i % 3]
        wait(dve, swap_of[i])
        rot_of[i] = stage("dve_rot").done(dve.tensor_tensor(rot, rot, qk_swap[i % 2], ALU.add))
        wait(act, rot_of[i], tr_of.get(i - 3))
        cast0_of[i] = stage("act_part").done(act.copy(part[:, 0, :], rot))

    def split(i):
        rot, part = qk_rot[i % 3], qk_part[i % 3]
        wait(dve, cast0_of[i])
        left0_of[i] = stage("dve_left").done(dve.tensor_tensor(rot, rot, part[:, 0, :], ALU.subtract))
        wait(act, left0_of[i])
        cast1_of[i] = stage("act_part").done(act.copy(part[:, 1, :], rot))
        wait(pool, cast1_of[i])
        part_of[i] = stage("pool_part").done(pool.tensor_tensor(part[:, 2, :], rot, part[:, 1, :], ALU.subtract))

    def transpose_parts(i):
        blk, at = divmod(i, TPB)
        wait(pe, part_of[i], evac_of.get(i - 1))
        tb = bank(2, 2).bitcast(BF16)
        part = qk_part[i % 3]
        for n in range(PARTS * 4):
            tr = pe.transpose(tb[:, n * P:(n + 1) * P], part[:, n // 4, (n % 4) * P:(n % 4 + 1) * P],
                              e.ident16[:])
        tr_of[i] = stage("pe_part_t").done(tr)
        wait(act, tr_of[i])
        if at == 0 and blk >= 2:
            wait(act, parts_written[blk - 2])
        evac_of[i] = stage("act_part_t").done(act.copy(
            part_t[blk % 2][:, :, at * P:(at + 1) * P],
            tb[:, 0:PARTS * 4 * P].rearrange("p (n q) -> p n q", q=P)))
        if at == TPB - 1:
            wait(sp, evac_of[i])
            parts_written.append(parts_out[blk % 2].done(sp.dma_start(
                parts_dram[:, :, blk * BLOCK:(blk + 1) * BLOCK].rearrange("n p q -> p n q"),
                part_t[blk % 2])))

    def projection_step(i):
        for lag, work_on in ((1, add_bias), (2, rotate), (3, split), (4, transpose_parts), (0, project)):
            if 0 <= i - lag < ALL_TILES:
                work_on(i - lag)

    stack_in = [e.dma_stage(f"stack_in{i}") for i in range(2)]
    stack_free = {}
    stacks = {}

    def load_stack(n, written):
        b, g = divmod(n, GROUPS)
        half = n % 2
        wait(sp, *written, *stack_free.get(n - 2, ()))
        tok = slice(b * SEQ, (b + 1) * SEQ)
        row0 = g * GROUP * DH
        for dst, which, order in ((k_stack[half], 1, K_PARTS), (q_stack[half], 0, Q_PARTS)):
            for slot, part in enumerate(order):
                src = parts_dram[part * 4 + which * CHUNKS + row0 // P, row0 % P:row0 % P + GROUP * DH, tok]
                mark = stack_in[half].done(sp.dma_start(
                    dst[slot * DH:(slot + 1) * DH, :, :], src.rearrange("(h d) n -> d h n", d=DH)))
        stacks[n] = mark

    max_of = []
    shift_in = [e.dma_stage(f"shift_in{i}") for i in range(2)]
    shift_rows = {}

    def find_maxima(n):
        qs, ks, found = q_stack[n % 2], k_stack[n % 2], row_max[n % 2]
        wait(pe, stacks[n], e.consts)
        for i in range(TILES):
            for j in range(GROUP):
                keys = (i + 1) * P
                for half, start in enumerate(range(0, keys, MAX_KEYS)):
                    turn = len(max_of)
                    if turn >= 2:
                        wait(pe, max_of[turn - 2])
                    unit = bank(4 + turn % 2 * 2, 2)
                    end = min(keys, start + MAX_KEYS)
                    if end == keys:
                        pe.matmul(unit[:, keys - P - start:keys - start], e.ident16[:], causal16[:],
                                  start=True, stop=False, skip_group_check=True)
                    for k0 in range(start, end, BLOCK):
                        width = min(BLOCK, end - k0)
                        mm = pe.matmul(unit[:, k0 - start:k0 - start + width],
                                       qs[0:SLOT_ROWS, j, i * P:(i + 1) * P],
                                       ks[0:SLOT_ROWS, j, k0:k0 + width],
                                       start=k0 + width < keys, stop=True, skip_group_check=True)
                        if k0 + width == end:
                            wait(dve, stage("pe_max").done(mm))
                            max_of.append(stage("dve_max").done(dve.tensor_reduce(
                                found[:, i, j, half:half + 1], unit[:, 0:end - start], AX.X, ALU.max)))
                        yield
        split_at = MAX_KEYS // P
        wait(dve, max_of[-1])
        stage("dve_shift").done(dve.tensor_reduce(
            shift[:, split_at:, :], found[:, split_at:, :, :], AX.X, ALU.max, negate=True))
        made = stage("dve_shift").done(dve.tensor_scalar(
            shift[:, 0:split_at, :], found[:, 0:split_at, :, 0], -1.0, None, ALU.mult))
        wait(dve, made, shift_read.get(n - 1))
        for part in range(PARTS):
            made = stage("dve_shift").done(dve.tensor_copy(shift16[:, :, part, :], shift[:]))
            if part < PARTS - 1:
                wait(dve, made)
                wait(dve, stage("dve_shift").done(dve.tensor_tensor(
                    shift[:], shift[:], shift16[:, :, part, :], ALU.subtract)))
        yield
        turn = len(max_of)
        wait(pe, made, max_of[turn - 2])
        tb = bank(4 + turn % 2 * 2, 2).bitcast(BF16)
        for i in range(TILES):
            tr = pe.transpose(tb[0:PARTS * GROUP, i * P:(i + 1) * P], shift16[:, i, :, :], e.ident16[:])
        shift_read[n] = stage("pe_shift_t").done(tr)
        wait(act, shift_read[n], shift_rows.get(n - 1))
        copied = stage("act_shift_t").done(act.copy(shift_t, tb[0:PARTS * GROUP, :]))
        max_of.append(copied)
        wait(sp, copied)
        for part in range(PARTS):
            shift_rows[n] = shift_in[n % 2].done(sp.dma_start(
                qs[SLOT_ROWS + part:SLOT_ROWS + part + 1, :, :].rearrange("p h n -> p (h n)"),
                shift_t[part * GROUP:(part + 1) * GROUP, :]))
        yield

    shift_read = {}
    MAX_STEPS = GROUP * sum(-(-(i + 1) // TPB) for i in range(TILES)) + 2

    unit_free = []
    exp_of, probs_read = {}, {}
    o_copied = []
    norm_of = []

    def next_unit():
        u = len(unit_free)
        if u >= SCORE_BANKS:
            wait(pe, unit_free[u - SCORE_BANKS])
        return bank(u % SCORE_BANKS)

    def attend(n, qb, kt, step):
        off = max(0, kt * P - qb * BLOCK)
        first, last = kt == (qb + 1) * TPB - 1, kt == 0
        b, g = divmod(n, GROUPS)
        for j in range(GROUP):
            wait(pe, *exp_of[step, j])
        if first and o_copied:
            wait(pe, o_copied[-1])
        for j in range(GROUP):
            col = (g * GROUP + j) * V_STRIDE
            mm = pe.matmul(bank(3)[j * COL_TILE:(j + 1) * COL_TILE, off:BLOCK],
                           v_aug[:, b * TILES + kt, col:col + COL_TILE],
                           probs[step % 2 * GROUP + j][:, off:BLOCK],
                           start=first, stop=last, skip_group_check=True)
        probs_read[step] = stage("pe_attn").done(mm)
        if last:
            turn = len(o_copied)
            wait(act, probs_read[step])
            if turn >= 2:
                wait(act, o_turned[turn - 2])
            o_copied.append(stage("act_o").done(act.copy(o_t[turn % 2], bank(3))))

    o_turned = []

    def turn_output(n, qb):
        b, g = divmod(n, GROUPS)
        turn = len(o_turned)
        unit = next_unit()
        wait(pe, o_copied[turn])
        for a in range(TPB):
            tr = pe.transpose(unit[:, a * P:(a + 1) * P], o_t[turn % 2][:, a * P:(a + 1) * P], e.ident[:])
        o_turned.append(stage("pe_o").done(tr))
        wait(dve, o_turned[turn])
        heads = unit.rearrange("p (n d) -> p n d", d=COL_TILE)
        rc = recip[turn % 2]
        wait(dve, stage("dve_norm").done(dve.reciprocal(rc[:], heads[:, :, DH])))
        tile0 = b * TILES + qb * TPB
        norm_of.append(stage("dve_norm").done(dve.tensor_tensor(
            e.tokens[:, tile0:tile0 + TPB, g * GROUP * DH:(g + 1) * GROUP * DH]
            .rearrange("p n (h d) -> p n h d", d=DH),
            heads[:, :, 0:DH].rearrange("p (n h) d -> p n h d", n=TPB),
            rc[:].rearrange("p (n h) -> p n h", n=TPB).unsqueeze(3).to_broadcast([P, TPB, GROUP, DH]),
            ALU.mult)))
        unit_free.append(norm_of[-1])

    steps = [(n, qb, kt) for n in range(ALL_GROUPS) for qb in range(BLOCKS)
             for kt in reversed(range((qb + 1) * TPB))]
    steps_of_group = len(steps) // ALL_GROUPS

    def score(step, side, ticks):
        n, qb, kt = steps[step]
        off = max(0, kt * P - qb * BLOCK)
        qs, ks = q_stack[n % 2], k_stack[n % 2]
        for j in range(GROUP):
            unit = next_unit()
            mm = pe.matmul(unit[:, off:BLOCK], ks[0:SCORE_ROWS, j, kt * P:(kt + 1) * P],
                           qs[0:SCORE_ROWS, j, qb * BLOCK + off:(qb + 1) * BLOCK], start=True, stop=True)
            scored = stage("pe_score").done(mm)
            pr = probs[step % 2 * GROUP + j]
            wait(act, scored, probs_read.get(step - 2))
            exp_done = stage("act_exp").done(act.activation(
                pr[:, off:BLOCK], unit[:, off:BLOCK], ACT.Exp, scale=SOFTMAX_SCALE))
            unit_free.append(exp_done)
            exp_of[step, j] = (exp_done,)
            if kt >= qb * TPB:
                wait(pool, exp_done)
                exp_of[step, j] = (stage("pool_causal").done(pool.affine_select(
                    out=pr[:, off:off + P], in_=pr[:, off:off + P], pattern=[[1, P]],
                    compare_op=ALU.is_ge, fill=0.0, base=0, channel_multiplier=-1)),)
            advance(side, ticks())
        return scored

    wait(pe, proj_in, e.ident_made)
    wait(dve, v_ones)
    wait(pool, proj_in)
    for i in range(TILES + 4):
        projection_step(i)
    load_stack(0, parts_written[-2:])
    maxima = find_maxima(0)
    for i in range(TILES + 4, ALL_TILES + 4):
        projection_step(i)
        if i >= TILES + 4 + PROJ_AHEAD:
            advance(maxima, -(-MAX_STEPS // (TILES - PROJ_AHEAD)))
    advance(maxima, MAX_STEPS)
    wait(dve, *parts_written[-2:])
    ones_rows = ones_made.done(dve.memset(k_stack[1][SLOT_ROWS:SLOT_ROWS + PARTS, :, :], 1.0))
    wait(pe, ones_rows, bias_of[ALL_TILES - 1], evac_of[ALL_TILES - 1])
    load_stack(1, parts_written[-2:])

    done_slots, side, owed = 0, iter(()), 0.0
    for step, (n, qb, kt) in enumerate(steps):
        at = step % steps_of_group
        if at == 0:
            advance(side, MAX_STEPS)
            wait(pe, shift_rows[n])
            side, owed = iter(()), 0.0
        if at == 1 and 0 < n < ALL_GROUPS - 1:
            load_stack(n + 1, ())
        if at == MAX_FROM and n < ALL_GROUPS - 1:
            side = find_maxima(n + 1)
        per_slot = MAX_STEPS / ((MAX_TO - MAX_FROM) * GROUP)

        def ticks():
            nonlocal owed
            owed += per_slot
            whole = int(owed)
            owed -= whole
            return whole

        scored = score(step, side, ticks)
        if step >= 1:
            attend(*steps[step - 1], step - 1)
            if len(o_turned) < len(o_copied) and step >= 2 and steps[step - 2][2] == 0:
                turn_output(*steps[step - 2][:2])
        if at == steps_of_group - 1:
            stack_free[n] = (scored,)
    attend(*steps[-1], len(steps) - 1)
    turn_output(*steps[-1][:2])
    e.attended = (norm_of[-1], probs_read[len(steps) - 1], exp_of[len(steps) - 1, GROUP - 1][0])


def emit_feed_forward(e, room):
    nc, t, bank, stage = e.nc, e.t, e.bank, e.stage
    pe, act, dve, pool, sp = nc.tensor, nc.scalar, nc.vector, nc.gpsimd, nc.sync
    tokens = e.tokens

    def sbuf(name, shape, dtype=F32):
        return e.sbuf(name, shape, dtype, room)

    x_res = [sbuf(f"x_res{i}", [P, TPB, DIM]) for i in range(2)]
    raw = {name: sbuf(name + "_raw", shape) for name, shape in (
        ("w_out", [P, CHUNKS, DIM]), ("w_router", [P, CHUNKS, EXPERTS]),
        ("w_gate", [P, CHUNKS, ALL_EXPERTS * INTER]), ("w_up", [P, CHUNKS, ALL_EXPERTS * INTER]),
        ("w_down", [P, ALL_EXPERTS, DIM]))}
    high = {name: sbuf(name + "_high", w.shape, F32R) for name, w in raw.items()}
    low = {name: sbuf(name + "_low", w.shape, F32R) for name, w in raw.items()}
    attn_high = [sbuf(f"attn_high{i}", [P, CHUNKS, P], F32R) for i in range(2)]
    attn_low = [sbuf(f"attn_low{i}", [P, CHUNKS, P], F32R) for i in range(2)]
    x1_high = [sbuf(f"x1_high{i}", [P, CHUNKS, BLOCK], F32R) for i in range(2)]
    x1_low = [sbuf(f"x1_low{i}", [P, CHUNKS, BLOCK], F32R) for i in range(2)]
    silu = [sbuf(f"silu{i}", [P, BLOCK]) for i in range(2)]
    hidden = [sbuf(f"hidden{i}", [P, BLOCK]) for i in range(2)]
    hid_high = [sbuf(f"hid_high{i}", [P, BLOCK], F32R) for i in range(2)]
    hid_low = [sbuf(f"hid_low{i}", [P, BLOCK], F32R) for i in range(2)]
    stats = sbuf("stats", [P, ALL_TILES, 6])
    mean_var = sbuf("mean_var", [P, ALL_TILES, 2])
    rstd = sbuf("rstd", [P, ALL_TILES])
    small = {name: sbuf("router_" + name, [P, TPB, EXPERTS], U32 if name == "top_at" else F32)
             for name in ("score", "top", "top_at", "top_atf", "pick", "pick2")}
    row_stat = sbuf("row_stat", [P, TPB])
    combine = [sbuf(f"combine{i}", [P, TPB, EXPERTS]) for i in range(2)]

    wait(sp, *e.attended)
    x_in = [e.dma_stage(f"x_in{i}") for i in range(2)]
    w_in = {name: e.dma_stage(name + "_in") for name in raw}
    b_out_in = e.dma_stage("b_out_in").done(sp.dma_start(e.b_out[:], t["b_out"]))
    loaded = {"w_out": w_in["w_out"].done(sp.dma_start(raw["w_out"][:], t["w_out"]))}
    x_marks = {}

    def load_x(blk):
        x_marks[blk] = x_in[blk % 2].done(sp.dma_start(
            x_res[blk % 2][:], t["x"][blk * BLOCK:(blk + 1) * BLOCK, :].rearrange("(n p) c -> p n c", p=P)))

    load_x(0)
    load_x(1)
    for name in list(raw)[1:]:
        loaded[name] = w_in[name].done(sp.dma_start(raw[name][:], t[name]))
    ready = {}

    def split_weight(name):
        wait(act, loaded[name], *e.attended)
        rounded = stage("act_w_high").done(act.copy(high[name][:], raw[name][:]))
        wait(pool, rounded)
        ready[name] = stage("pool_w_low").done(
            pool.tensor_tensor(low[name][:], raw[name][:], high[name][:], ALU.subtract))

    def product(out, lhs, rhs, start=True, stop=True):
        pe.matmul(out, lhs[0], rhs[0], start=start, stop=False)
        pe.matmul(out, lhs[0], rhs[1], start=False, stop=False)
        return pe.matmul(out, lhs[1], rhs[0], start=False, stop=stop)

    wait(act, *e.attended)
    wait(dve, *e.attended)
    wait(pool, *e.attended)
    wait(pe, *e.attended)
    split_weight("w_out")
    turned_of, high_of, low_of, res_of, out_of, biased_of = ({} for _ in range(6))
    ln1_of = {}

    def turn_attention(i):
        blk, at = divmod(i, TPB)
        buf = i % 2
        if at == 0:
            if blk >= 2:
                wait(sp, res_of[(blk - 1) * TPB - 1])
                load_x(blk)
            wait(pool, x_marks[blk], b_out_in)
            for a in range(TPB):
                biased_of[blk] = stage("pool_bias").done(pool.tensor_tensor(
                    x_res[blk % 2][:, a, :], x_res[blk % 2][:, a, :], e.b_out[:], ALU.add))
        wait(pe, low_of.get(i - 2))
        for c in range(CHUNKS):
            tr = pe.transpose(bank(buf)[:, c * P:(c + 1) * P], tokens[:, i, c * P:(c + 1) * P], e.ident[:])
        turned_of[i] = stage("pe_attn_t").done(tr)
        src = bank(buf)[:, 0:DIM].rearrange("p (c q) -> p c q", c=CHUNKS)
        wait(act, turned_of[i], out_of.get(i - 2))
        high_of[i] = stage("act_attn_high").done(act.copy(attn_high[buf][:], src))
        wait(dve, high_of[i])
        low_of[i] = stage("dve_attn_low").done(
            dve.tensor_tensor(attn_low[buf][:], src, attn_high[buf][:], ALU.subtract))

    def output_product(i):
        blk, at = divmod(i, TPB)
        buf = i % 2
        wait(pe, low_of[i], res_of.get(i - 2))
        for c in range(CHUNKS):
            mm = product(bank(2 + buf)[:, 0:DIM], (attn_high[buf][:, c, :], attn_low[buf][:, c, :]),
                         (high["w_out"][:, c, :], low["w_out"][:, c, :]), c == 0, c == CHUNKS - 1)
        out_of[i] = stage("pe_out").done(mm)
        wait(dve, out_of[i], biased_of[blk])
        res_of[i] = stage("dve_res").done(dve.tensor_tensor(
            tokens[:, i, :], bank(2 + buf)[:, 0:DIM], x_res[blk % 2][:, at, :], ALU.add))

    def statistics(i, tag):
        wait(dve, stage("dve_ln").done(dve.bn_stats(stats[:, i, :], tokens[:, i, :])))
        return stage("dve_ln").done(dve.bn_aggr(mean_var[:, i, :], stats[:, i, :]))

    def inverse_deviation(tiles, known):
        wait(act, known, e.consts)
        root = stage("act_sqrt").done(act.activation(rstd[:, tiles], mean_var[:, tiles, 1], ACT.Sqrt,
                                                     bias=e.eps[:]))
        wait(dve, root)
        return stage("dve_ln").done(dve.reciprocal(rstd[:, tiles], rstd[:, tiles]))

    def normalise(i):
        return stage("dve_ln").done(dve.tensor_scalar(
            tokens[:, i, :], tokens[:, i, :], mean_var[:, i, 0:1], rstd[:, i:i + 1],
            ALU.subtract, ALU.mult))

    wait(pe, ready["w_out"])
    for i in range(ALL_TILES + 2):
        if i < ALL_TILES:
            turn_attention(i)
        if 1 <= i <= ALL_TILES:
            output_product(i - 1)
        if i >= 2:
            wait(dve, res_of[i - 2])
            known = statistics(i - 2, "ln1")
        if i == 4:
            for name in list(raw)[1:]:
                split_weight(name)
        if i - 2 in (TILES - 1, ALL_TILES - 1):
            first = i - 2 - TILES + 1
            wait(dve, inverse_deviation(slice(first, first + TILES), known))
            for a in range(first, first + TILES):
                ln1_of[a] = normalise(a)

    for name in list(raw)[1:]:
        wait(pe, ready[name])
    combined_of, x1_of, logits_read = {}, {}, {}
    h_of, low_h_of, silu_of, down_of, y_of = {}, {}, {}, {}, {}
    jobs = [(blk, k) for blk in range(ALL_BLOCKS) for k in range(ALL_EXPERTS)]
    r = stage("dve_router")

    def prepare(blk):
        half = blk % 2
        if blk >= 2:
            last_read = up_of[(blk - 1) * ALL_EXPERTS - 1]
            wait(act, last_read)
            wait(dve, last_read)
        for a in range(TPB):
            i = blk * TPB + a
            wait(pe, ln1_of[i], x1_of.get(i - 1))
            for c in range(CHUNKS):
                tr = pe.transpose(bank(6)[:, c * P:(c + 1) * P], tokens[:, i, c * P:(c + 1) * P], e.ident[:])
            wait(act, stage("pe_x1_t").done(tr))
            src = bank(6)[:, 0:DIM].rearrange("p (c q) -> p c q", c=CHUNKS)
            rounded = stage("act_x1_high").done(act.copy(x1_high[half][:, :, a * P:(a + 1) * P], src))
            wait(dve, rounded)
            x1_of[i] = stage("dve_x1_low").done(dve.tensor_tensor(
                x1_low[half][:, :, a * P:(a + 1) * P], src, x1_high[half][:, :, a * P:(a + 1) * P],
                ALU.subtract))
            yield
        logits = bank(7)[:, 0:TPB * EXPERTS].rearrange("p (n k) -> p n k", k=EXPERTS)
        wait(pe, x1_of[blk * TPB + TPB - 1], logits_read.get(blk - 1))
        for a in range(TPB):
            for c in range(CHUNKS):
                at = slice(a * P, (a + 1) * P)
                mm = product(logits[:, a, :], (x1_high[half][:, c, at], x1_low[half][:, c, at]),
                             (high["w_router"][:, c, :], low["w_router"][:, c, :]),
                             c == 0, c == CHUNKS - 1)
        scored = stage("pe_router").done(mm)
        yield

        def over_experts(ap):
            return ap.unsqueeze(2).to_broadcast([P, TPB, EXPERTS])

        v = {name: buf[:] for name, buf in small.items()}
        wait(dve, scored)
        wait(dve, r.done(dve.tensor_reduce(row_stat[:], logits, AX.X, ALU.max)))
        logits_read[blk] = r.done(dve.tensor_tensor(v["score"], logits, over_experts(row_stat[:]), ALU.subtract))
        wait(act, logits_read[blk])
        powers = stage("act_router").done(act.activation(v["score"], v["score"], ACT.Exp))
        yield
        wait(dve, powers)
        wait(dve, r.done(dve.tensor_reduce(row_stat[:], v["score"], AX.X, ALU.add)))
        wait(dve, r.done(dve.reciprocal(row_stat[:], row_stat[:])))
        wait(dve, r.done(dve.tensor_tensor(v["score"], v["score"], over_experts(row_stat[:]), ALU.mult)))
        yield
        for a in range(TPB):
            m = r.done(dve.max(v["top"][:, a, :], v["score"][:, a, :]))
        wait(dve, m)
        for a in range(TPB):
            m = r.done(dve.max_index(v["top_at"][:, a, :], v["top"][:, a, :], v["score"][:, a, :]))
        wait(dve, m)
        yield
        wait(dve, r.done(dve.tensor_copy(v["top_atf"], v["top_at"])))
        ids = e.expert_ids[:].unsqueeze(1).to_broadcast([P, TPB, EXPERTS])
        for k, dst in ((0, v["pick"]), (1, v["pick2"])):
            m = r.done(dve.tensor_tensor(dst, ids, over_experts(v["top_atf"][:, :, k]), ALU.is_equal))
        wait(dve, m)
        wait(dve, r.done(dve.tensor_tensor(v["pick"], v["pick"], v["pick2"], ALU.add)))
        combined_of[blk] = r.done(dve.tensor_tensor(combine[half][:], v["pick"], v["score"], ALU.mult))
        yield

    up_of = {}

    def gate_up(n):
        blk, k = jobs[n]
        buf, half = n % 2, blk % 2
        cols = slice(k * INTER, (k + 1) * INTER)
        wait(pe, h_of.get(n - 2))
        for dst, name in ((bank(buf), "w_gate"), (bank(2 + buf), "w_up")):
            for c in range(CHUNKS):
                mm = product(dst, (high[name][:, c, cols], low[name][:, c, cols]),
                             (x1_high[half][:, c, :], x1_low[half][:, c, :]), c == 0, c == CHUNKS - 1)
            if name == "w_gate":
                wait(act, stage("pe_gate").done(mm), h_of.get(n - 2))
                silu_of[n] = stage("act_silu").done(act.activation(silu[buf][:], bank(buf), ACT.Silu))
        up_of[n] = stage("pe_up").done(mm)
        wait(dve, up_of[n], silu_of[n], low_h_of.get(n - 2))
        h_of[n] = stage("dve_h").done(dve.tensor_tensor(hidden[buf][:], bank(2 + buf), silu[buf][:], ALU.mult))
        wait(act, h_of[n], down_of.get(n - 2))
        rounded = stage("act_h_high").done(act.copy(hid_high[buf][:], hidden[buf][:]))
        wait(pool, rounded, down_of.get(n - 2))
        low_h_of[n] = stage("pool_h_low").done(
            pool.tensor_tensor(hid_low[buf][:], hidden[buf][:], hid_high[buf][:], ALU.subtract))

    def down(n):
        blk, k = jobs[n]
        buf = n % 2
        wait(pe, low_h_of[n])
        for pair in range(TPB // 2):
            wait(pe, y_of.get((n - 1, pair)))
            for a in range(2):
                at = slice((pair * 2 + a) * P, (pair * 2 + a + 1) * P)
                mm = product(bank(4 + pair)[:, a * DIM:(a + 1) * DIM],
                             (hid_high[buf][:, at], hid_low[buf][:, at]),
                             (high["w_down"][:, k, :], low["w_down"][:, k, :]))
            down_of[n] = stage("pe_down").done(mm)
            wait(dve, down_of[n], y_of.get((n - 1, pair)))
            if k == 1:
                wait(dve, combined_of[blk])
            for a in range(2):
                i = blk * TPB + pair * 2 + a
                y = bank(4 + pair)[:, a * DIM:(a + 1) * DIM]
                if k == 0:
                    op = dve.tensor_tensor(tokens[:, i, :], y, tokens[:, i, :], ALU.add)
                else:
                    op = dve.scalar_tensor_tensor(
                        out=tokens[:, i, :], in0=y, scalar=combine[blk % 2][:, pair * 2 + a, k - 1:k],
                        in1=tokens[:, i, :], op0=ALU.mult, op1=ALU.add)
            y_of[n, pair] = stage("dve_y").done(op)

    stores = []
    y_out = [e.dma_stage(f"y_out{i}") for i in range(ALL_BLOCKS)]

    def finish(blk):
        tiles = range(blk * TPB, (blk + 1) * TPB)
        wait(dve, y_of[(blk + 1) * ALL_EXPERTS - 1, TPB // 2 - 1])
        for i in tiles:
            known = statistics(i, "ln2")
            yield
        wait(dve, inverse_deviation(slice(tiles[0], tiles[0] + TPB), known))
        for i in tiles:
            m = normalise(i)
        wait(sp, m)
        stores.append(y_out[blk].done(sp.dma_start(
            t["out"][blk * BLOCK:(blk + 1) * BLOCK, :].rearrange("(n p) c -> p n c", p=P),
            tokens[:, tiles[0]:tiles[0] + TPB, :])))
        yield

    advance(prepare(0), 99)
    chores = iter(())
    for n in range(len(jobs) + 1):
        if n < len(jobs):
            blk, k = jobs[n]
            if k == 0 and n:
                advance(chores, 99)
            wait(pe, x1_of[blk * TPB + TPB - 1])
            gate_up(n)
            advance(chores)
        if n >= 1:
            down(n - 1)
            if jobs[n - 1][1] == ALL_EXPERTS - 1:
                finished = jobs[n - 1][0]
                if finished == ALL_BLOCKS - 1:
                    advance(finish(finished), 99)
                else:
                    chores = chain(finish(finished), prepare_next(finished + 2, prepare))
            if n == 1:
                chores = prepare(1)
            advance(chores)

    wait(sp, *stores)


def prepare_next(blk, prepare):
    if blk < ALL_BLOCKS:
        yield from prepare(blk)


def rotation_tables():
    f = np.float32
    pos = np.arange(SEQ, dtype=f)
    inv_freq = (f(1.0) / f(10000.0) ** (np.arange(0, DH, 2, dtype=f) / f(DH))).astype(f)
    freqs = np.repeat(pos[:, None] * inv_freq[None, :], 2, axis=-1)
    cos, sin = np.cos(freqs), np.sin(freqs)
    base = (np.arange(0, DH, 2, dtype=f) + f(0.4 * DH)) / f(1.4 * DH)
    power = (pos - f(SEQ // 2)) / f(512.0)
    scale = base[None, :] ** power[:, None]
    scale = np.concatenate((scale, scale), axis=-1).astype(f)
    sign = np.where(np.arange(DH) % 2 == 0, f(-1.0), f(1.0))[None, :]
    both = np.stack((scale, f(1.0) / scale), axis=1)
    cos_t, sin_t = cos[:, None, :] * both, (sin * sign)[:, None, :] * both

    def tiled(a):
        return np.ascontiguousarray(a.reshape(TILES, P, 2, DH).transpose(1, 0, 2, 3).astype(f))

    return tiled(cos_t), tiled(sin_t)


def kernel(L0_attn_x, L0_attn_Wq, L0_attn_bq, L0_attn_Wk, L0_attn_bk, L0_attn_Wv, L0_attn_bv,
           L0_attn_Wo, L0_attn_bo, L0_ffn_gate_w, L0_ffn_wg, L0_ffn_wu, L0_ffn_wd, L0_ffn_sg,
           L0_ffn_su, L0_ffn_sd):
    import concourse.bacc as bacc
    from concourse.bass_utils import run_bass_kernel_spmd

    def chunked(w):
        return w.reshape(-1, P, w.shape[-1]).transpose(1, 0, 2)

    def rows(v):
        return np.broadcast_to(v[None, :], (P, v.shape[0]))

    x = np.asarray(L0_attn_x).reshape(BATCH * SEQ, DIM)
    w_qkv = np.concatenate([np.asarray(w).T for w in (L0_attn_Wq, L0_attn_Wv, L0_attn_Wk)], axis=1)
    b_qkv = np.concatenate([np.asarray(v) for v in (L0_attn_bq, L0_attn_bv, L0_attn_bk)])
    gate = np.concatenate([np.asarray(L0_ffn_sg)[None], np.asarray(L0_ffn_wg)]).reshape(-1, DIM).T
    up = np.concatenate([np.asarray(L0_ffn_su)[None], np.asarray(L0_ffn_wu)]).reshape(-1, DIM).T
    down = np.concatenate([np.asarray(L0_ffn_sd)[None], np.asarray(L0_ffn_wd)]).transpose(2, 0, 1)
    cos_t, sin_t = rotation_tables()
    arrays = {
        "x": x, "x_t": x.T, "w_qkv": chunked(w_qkv), "b_qkv": rows(b_qkv),
        "rot_cos": cos_t, "rot_sin": sin_t, "ident": np.eye(P, dtype=np.float32),
        "w_out": chunked(np.asarray(L0_attn_Wo).T), "b_out": rows(np.asarray(L0_attn_bo)),
        "w_router": chunked(np.asarray(L0_ffn_gate_w).T), "w_gate": chunked(gate),
        "w_up": chunked(up), "w_down": down,
    }
    arrays = {k: np.ascontiguousarray(v) for k, v in arrays.items()}
    nc = bacc.Bacc("TRN2", target_bir_lowering=False, num_devices=1)
    tensors = {k: nc.dram_tensor(k + "_dram", v.shape, mybir.dt.from_np(v.dtype), kind="ExternalInput").ap()
               for k, v in arrays.items()}
    tensors["parts_dram"] = nc.dram_tensor("parts_scratch", (PARTS * 4, P, BATCH * SEQ), BF16, kind="Internal").ap()
    tensors["out"] = nc.dram_tensor("out_dram", (BATCH * SEQ, DIM), F32, kind="ExternalOutput").ap()
    build_program(nc, tensors)
    result = run_bass_kernel_spmd(nc, [{k + "_dram": v for k, v in arrays.items()}], core_ids=[0])
    return result.results[0]["out_dram"].reshape(BATCH, SEQ, DIM)
```

```python
from contextlib import ExitStack
from itertools import chain

import numpy as np

import concourse.bass as bass
from concourse import mybir
from concourse.alu_op_type import AluOpType as ALU

ACT = mybir.ActivationFunctionType
AX = mybir.AxisListType
F32 = mybir.dt.float32
BF16 = mybir.dt.bfloat16
U32 = mybir.dt.uint32
F32R = mybir.dt.float32r

P = 128
BATCH, SEQ, DIM = 2, 2048, 256
HEADS, DH = 16, 16
EXPERTS, INTER = 8, 128
ALL_EXPERTS = EXPERTS + 1
TILES = SEQ // P
BLOCK = 512
BLOCKS = SEQ // BLOCK
TPB = BLOCK // P
CHUNKS = DIM // P
GROUP = 4
GROUPS = HEADS // GROUP
PARTS = 3
QK = 2 * DIM
Q_PARTS = (0, 0, 1, 1, 0, 2)
K_PARTS = (0, 1, 0, 1, 2, 0)
SLOT_ROWS = DH * len(Q_PARTS)
SCORE_ROWS = SLOT_ROWS + PARTS
V_STRIDE = DH + 1
COL_TILE = 32
V_COLS = (HEADS - 1) * V_STRIDE + COL_TILE
ALL_TILES = BATCH * TILES
ALL_BLOCKS = BATCH * BLOCKS
ALL_GROUPS = BATCH * GROUPS
BANK = 512
BANKS = 8
SCORE_BANKS = 3
MAX_BANKS = 4
SHIFT_LAG = 8
EPS = 1e-5
SOFTMAX_SCALE = 1.0 / (DH * HEADS) ** 0.5
MASKED = -1e30
ONES_COLS = 256
ONES_ROWS = GROUP * SEQ // ONES_COLS
REDUCE_COST = 80
TURN_COST, PRODUCT_COST = 2 * BLOCK, 2 * BLOCK
PROJ_AHEAD = 6
SIDE_STEPS = 2
DRAIN_STEPS = 3
EARLY_GROUPS = 1
EARLY_PACE = 1.2
MAX_SHARE = 0.7
SHIFTS_AHEAD = 2
SIDE_PACE = 0.98
NORMALISE_AT = ALL_EXPERTS - 4
STACKS = 3


class Stage:

    def __init__(self, ctx, nc, name, step=1):
        self.sem = ctx.enter_context(nc.semaphore(name))
        self.step = step
        self.count = 0

    def done(self, instruction):
        self.count += self.step
        instruction.then_inc(self.sem, self.step)
        return self.sem, self.count


def wait(engine, *marks):
    for mark in marks:
        if mark is not None:
            engine.wait_ge(*mark)


def build_program(nc, t):
    with ExitStack() as ctx:
        e = Emitter(nc, t, ctx)
        with ExitStack() as early, ExitStack() as attention:
            late = ctx.enter_context(ExitStack())
            emit_attention(e, early, attention, late)
        e.experts.after_attention()


class Emitter:

    def __init__(self, nc, t, ctx):
        self.nc, self.t, self.ctx = nc, t, ctx
        self.stages = {}
        self.block_attended = {}
        self.psum = ctx.enter_context(nc.psum_tensor("psum", [P, BANKS * BANK], F32))
        self.ident = self.sbuf("ident", [P, P])
        self.ident16 = self.sbuf("ident16", [P, P], BF16)
        self.tokens = self.sbuf("tokens", [P, ALL_TILES, DIM])
        self.b_out = self.sbuf("b_out", [P, DIM])
        self.eps = self.sbuf("eps", [P, 1])
        self.expert_ids = self.sbuf("expert_ids", [P, EXPERTS])

    def sbuf(self, name, shape, dtype=F32, room=None, side="left"):
        return (room or self.ctx).enter_context(self.nc.sbuf_tensor(name, shape, dtype, side=side))

    def bank(self, i, n=1):
        return self.psum[:, i * BANK:(i + n) * BANK]

    def stage(self, name):
        if name not in self.stages:
            self.stages[name] = Stage(self.ctx, self.nc, name)
        return self.stages[name]

    def dma_stage(self, name):
        if name not in self.stages:
            self.stages[name] = Stage(self.ctx, self.nc, name, 16)
        return self.stages[name]


def advance(work, steps=1):
    for _ in range(steps):
        next(work, None)


def emit_attention(e, early, attention, late):
    nc, t, bank, stage = e.nc, e.t, e.bank, e.stage
    pe, act, dve, pool, sp = nc.tensor, nc.scalar, nc.vector, nc.gpsimd, nc.sync

    def sbuf(name, shape, dtype=F32):
        return e.sbuf(name, shape, dtype, attention, "right")

    ones16 = sbuf("ones16", [ONES_ROWS, ONES_COLS], BF16)
    causal16 = sbuf("causal16", [P, P], BF16)
    probs = [sbuf(f"probs{i}", [P, BLOCK]) for i in range(2 * GROUP)]
    row_max = sbuf("row_max", [P, 2, TPB, GROUP, BLOCKS])
    shift = sbuf("shift", [P, TPB, GROUP])
    shift16 = sbuf("shift16", [P, TPB, PARTS, GROUP], BF16)
    shift_t = [sbuf(f"shift_t{i}", [PARTS * GROUP, BLOCK], BF16) for i in range(2)]
    recip = [sbuf(f"recip{i}", [P, TPB * GROUP]) for i in range(2)]
    o_t = [sbuf(f"o_t{i}", [P, BLOCK])[:] for i in range(2)]

    q_stack, k_stack = [None] * STACKS, [None] * STACKS

    def make_stack(i, room, side):
        q_stack[i] = e.sbuf(f"q_stack{i}", [P, GROUP, SEQ], BF16, room, side)
        k_stack[i] = e.sbuf(f"k_stack{i}", [P, GROUP, SEQ], BF16, room, side)

    v_aug = [e.sbuf("v_aug0", [P, TILES, V_COLS], F32, early, "left"), sbuf("v_aug1", [P, TILES, V_COLS])]
    make_stack(1, attention, "right")
    make_stack(0, early, "left")
    part_t = [stack[:].rearrange("p h n -> p (h n)")[:, 0:PARTS * 4 * BLOCK]
              .rearrange("p (n q) -> p n q", q=BLOCK) for stack in (q_stack[1], k_stack[1])]

    proj = ExitStack()
    w_qkv = e.sbuf("w_qkv", [P, CHUNKS, 3 * DIM], F32, proj)
    b_qkv = e.sbuf("b_qkv", [P, 3 * DIM], F32, proj)
    rot_cos = e.sbuf("rot_cos", [P, TILES, 2, DH], F32, proj)
    rot_sin = e.sbuf("rot_sin", [P, TILES, 2, DH], F32, proj)
    x_t = [e.sbuf(f"x_t{i}", [P, CHUNKS, BLOCK], F32, proj) for i in range(2)]
    work = e.tokens[:].rearrange("p n c -> p (n c)")
    qk_raw = [work[:, i * QK:(i + 1) * QK] for i in range(2)]
    qk_swap = [work[:, (2 + i) * QK:(3 + i) * QK] for i in range(2)]
    qk_rot = [work[:, (4 + i) * QK:(5 + i) * QK] for i in range(4)]
    part_at, part_room = 8 * QK, PARTS * QK // 2
    qk_part = [work[:, part_at + i * part_room:part_at + (i + 1) * part_room].bitcast(BF16)
               .rearrange("p (n c) -> p n c", n=PARTS) for i in range(4)]

    proj_in = None
    xt_in = [e.dma_stage(f"xt_in{i}") for i in range(2)]
    weights_in = e.dma_stage("weights_in")

    def load_x_t(blk):
        return xt_in[blk % 2].done(act.dma_start(
            x_t[blk % 2][:], t["x_t"][:, blk * BLOCK:(blk + 1) * BLOCK].rearrange("(c p) n -> p c n", p=P)))

    xt_marks = {}
    x_t_src = t["x_t"].rearrange("(c p) n -> p c n", p=P)
    first_tile_in = e.dma_stage("first_tile_in").done(sp.dma_start(x_t[0][:, :, 0:P], x_t_src[:, :, 0:P]))
    w_qk_in = [e.dma_stage(f"w_qk_in{c}").done(queue.dma_start(w_qkv[:, c, 0:QK], t["w_qkv"][:, c, 0:QK]))
               for c, queue in enumerate((act, sp))]
    xt_marks[0] = xt_in[0].done(sp.dma_start(x_t[0][:, :, P:BLOCK], x_t_src[:, :, P:BLOCK]))
    w_v_in = e.dma_stage("w_v_in").done(act.dma_start(w_qkv[:, :, QK:3 * DIM], t["w_qkv"][:, :, QK:3 * DIM]))
    for buf, name in ((b_qkv, "b_qkv"), (rot_cos, "rot_cos"), (rot_sin, "rot_sin"), (e.ident, "ident")):
        proj_in = weights_in.done(act.dma_start(buf[:], t[name]))
    xt_marks[1] = load_x_t(1)

    const_made = stage("const_made")
    ones_made = const_made.done(pool.memset(ones16[:], 1.0))
    zeros_made = const_made.done(pool.memset(causal16[:], 0.0))
    v_ones = [const_made.done(pool.memset(v[:], 1.0)) for v in v_aug]
    const_made.done(pool.memset(e.eps[:], EPS))
    for k in range(EXPERTS):
        const_made.done(pool.memset(e.expert_ids[:, k:k + 1], float(k)))
    wait(pool, zeros_made)
    e.consts = const_made.done(pool.affine_select(
        out=causal16[:], in_=causal16[:], pattern=[[-1, P]], compare_op=ALU.is_ge, fill=MASKED,
        base=0, channel_multiplier=1))
    wait(dve, proj_in)
    e.ident_made = stage("ident_cast").done(dve.tensor_copy(e.ident16[:], e.ident[:]))

    parts_out = [e.dma_stage(f"parts_out{i}") for i in range(2)]
    parts_dram = t["parts_dram"]
    qk_of, v_of, raw_of, bias_of, swap_of, rot_of, cast0_of, cast1_of, part_of, tr_of, evac_of = ({} for _ in range(11))
    left0_of = {}
    parts_written = []

    def project(i):
        blk, at = divmod(i, TPB)
        if at == 1 and blk >= 1 and blk + 1 < ALL_BLOCKS:
            wait(act, v_of[blk * TPB - 1])
            xt_marks[blk + 1] = load_x_t(blk + 1)
        wait(pe, xt_marks[blk] if i else first_tile_in, raw_of.get(i - 1))
        lhs = [x_t[blk % 2][:, c, at * P:(at + 1) * P] for c in range(CHUNKS)]
        for c in range(CHUNKS):
            wait(pe, w_qk_in[c])
            mm = pe.matmul(bank(0)[:, 0:QK], lhs[c], w_qkv[:, c, 0:QK], start=(c == 0), stop=(c == CHUNKS - 1))
        qk_of[i] = stage("pe_qk").done(mm)
        wait(pe, w_v_in, bias_of.get(i - 1))
        for c in range(CHUNKS):
            mm = pe.matmul(bank(1)[:, 0:DIM], lhs[c], w_qkv[:, c, QK:QK + DIM],
                           start=(c == 0), stop=(c == CHUNKS - 1))
        v_of[i] = stage("pe_v").done(mm)

    def add_bias(i):
        raw, swp, rot = qk_raw[i % 2], qk_swap[i % 2], qk_rot[i % 4]
        wait(dve, qk_of[i], swap_of.get(i - 2))
        raw_of[i] = stage("dve_bias").done(dve.tensor_tensor(raw, bank(0)[:, 0:QK], b_qkv[:, 0:QK], ALU.add))
        wait(dve, v_of[i], v_ones[i // TILES])
        bias_of[i] = stage("dve_bias").done(dve.tensor_tensor(
            v_aug[i // TILES][:, i % TILES, 0:HEADS * V_STRIDE].rearrange("p (h d) -> p h d", h=HEADS)[:, :, 0:DH],
            bank(1)[:, 0:DIM].rearrange("p (h d) -> p h d", h=HEADS),
            b_qkv[:, QK:QK + DIM].rearrange("p (h d) -> p h d", h=HEADS), ALU.add))
        wait(pool, raw_of[i], rot_of.get(i - 2), part_of.get(i - 4))
        pool.tensor_tensor(
            rot.rearrange("p (a h d) -> p a h d", a=2, h=HEADS),
            raw.rearrange("p (a h d) -> p a h d", a=2, h=HEADS),
            rot_cos[:, i % TILES, :, :].unsqueeze(2).to_broadcast([P, 2, HEADS, DH]), ALU.mult)
        pair = "p (a h f e) -> p a h f e"
        raw5 = raw.rearrange(pair, a=2, h=HEADS, e=2)
        swp5 = swp.rearrange(pair, a=2, h=HEADS, e=2)
        sin4 = rot_sin[:, i % TILES, :, :].rearrange("p a (f e) -> p a f e", e=2)
        for k in range(2):
            op = pool.tensor_tensor(
                swp5[:, :, :, :, k], raw5[:, :, :, :, 1 - k],
                sin4[:, :, :, k].unsqueeze(2).to_broadcast([P, 2, HEADS, DH // 2]), ALU.mult)
        swap_of[i] = stage("pool_rot").done(op)

    def rotate(i):
        rot, part = qk_rot[i % 4], qk_part[i % 4]
        wait(dve, swap_of[i])
        rot_of[i] = stage("dve_rot").done(dve.tensor_tensor(rot, rot, qk_swap[i % 2], ALU.add))
        wait(act, rot_of[i], tr_of.get(i - 4))
        cast0_of[i] = stage("act_part").done(act.copy(part[:, 0, :], rot))

    def split(i):
        rot, part = qk_rot[i % 4], qk_part[i % 4]
        wait(dve, cast0_of[i])
        left0_of[i] = stage("dve_left").done(dve.tensor_tensor(rot, rot, part[:, 0, :], ALU.subtract))
        wait(act, left0_of[i])
        cast1_of[i] = stage("act_part").done(act.copy(part[:, 1, :], rot))

    def split_last(i):
        wait(dve, cast1_of[i])
        part_of[i] = stage("dve_part").done(dve.tensor_tensor(
            qk_part[i % 4][:, 2, :], qk_rot[i % 4], qk_part[i % 4][:, 1, :], ALU.subtract))

    def transpose_parts(i):
        blk, at = divmod(i, TPB)
        wait(pe, part_of[i], evac_of.get(i - 1), e.ident_made if i == 0 else None)
        tb = bank(2, 2).bitcast(BF16)
        part = qk_part[i % 4]
        for n in range(PARTS * 4):
            tr = pe.transpose(tb[:, n * P:(n + 1) * P], part[:, n // 4, (n % 4) * P:(n % 4 + 1) * P],
                              e.ident16[:])
        tr_of[i] = stage("pe_part_t").done(tr)
        wait(act, tr_of[i])
        if at == 0 and blk >= 2:
            wait(act, parts_written[blk - 2])
        evac_of[i] = stage("act_part_t").done(act.copy(
            part_t[blk % 2][:, :, at * P:(at + 1) * P],
            tb[:, 0:PARTS * 4 * P].rearrange("p (n q) -> p n q", q=P)))
        if at == TPB - 1:
            wait(sp, evac_of[i])
            parts_written.append(parts_out[blk % 2].done(sp.dma_start(
                parts_dram[:, :, blk * BLOCK:(blk + 1) * BLOCK].rearrange("n p q -> p n q"),
                part_t[blk % 2])))

    pipeline = ((0, project), (4, transpose_parts), (0, add_bias), (1, rotate), (2, split), (3, split_last))
    drain = 4

    def projection_step(i, side=iter(())):
        for lag, work_on in pipeline:
            if 0 <= i - lag < ALL_TILES:
                work_on(i - lag)
            if work_on in (transpose_parts, rotate, split_last):
                advance(side, SIDE_STEPS if i < ALL_TILES else DRAIN_STEPS)

    stack_in = [e.dma_stage(f"stack_in{i}") for i in range(STACKS)]
    stack_free = {}
    stacks = {}

    def load_stack(n, written):
        b, g = divmod(n, GROUPS)
        half = n % STACKS
        wait(sp, *written, *stack_free.get(n - STACKS, ()))
        tok = slice(b * SEQ, (b + 1) * SEQ)
        row0 = g * GROUP * DH
        for dst, which, order in ((k_stack[half], 1, K_PARTS), (q_stack[half], 0, Q_PARTS)):
            for slot, part in enumerate(order):
                src = parts_dram[part * 4 + which * CHUNKS + row0 // P, row0 % P:row0 % P + GROUP * DH, tok]
                mark = stack_in[half].done(sp.dma_start(
                    dst[slot * DH:(slot + 1) * DH, :, :], src.rearrange("(h d) n -> d h n", d=DH)))
        for row in range(SLOT_ROWS, SCORE_ROWS):
            mark = stack_in[half].done(sp.dma_start(
                k_stack[half][row:row + 1, :, :].rearrange("r h (a c) -> r (h a) c", c=ONES_COLS), ones16[:]))
        stacks[n] = mark

    max_read = []
    shift_in = [e.dma_stage(f"shift_in{i}") for i in range(2)]
    shift_read, shift_rows = {}, {}

    def max_unit():
        turn = len(max_read)
        if turn >= MAX_BANKS:
            wait(pe, max_read[turn - MAX_BANKS])
        return bank(4 + turn % MAX_BANKS)

    def before(n, qb, back):
        return divmod(n * BLOCKS + qb - back, BLOCKS)

    def find_maxima(n, qb):
        qs, ks = q_stack[n % STACKS], k_stack[n % STACKS]
        if qb == 0:
            wait(pe, stacks[n], e.consts)
        found = row_max[:, qb % 2, :, :, :]
        for a in range(TPB):
            i = qb * TPB + a
            for kb in range(qb + 1):
                width = BLOCK if kb < qb else (a + 1) * P
                heads = 1 << (BLOCK // width).bit_length() - 1
                for first in range(0, GROUP, heads):
                    unit = max_unit()
                    for j in range(first, first + heads):
                        at = unit[:, (j - first) * width:(j - first + 1) * width]
                        if kb == qb:
                            pe.matmul(at[:, width - P:width], e.ident16[:], causal16[:],
                                      start=True, stop=False, skip_group_check=True)
                        mm = pe.matmul(at, qs[0:SLOT_ROWS, j, i * P:(i + 1) * P],
                                       ks[0:SLOT_ROWS, j, kb * BLOCK:kb * BLOCK + width],
                                       start=kb < qb, stop=True, skip_group_check=True)
                    wait(dve, stage("pe_max").done(mm))
                    max_read.append(stage("dve_max").done(dve.tensor_reduce(
                        found[:, a, first:first + heads, kb],
                        unit[:, 0:heads * width].rearrange("p (h n) -> p h n", h=heads), AX.X, ALU.max)))
                    yield heads * width + REDUCE_COST
        wait(dve, max_read[-1])
        made = stage("dve_shift").done(dve.tensor_reduce(
            shift[:], found[:, :, :, 0:qb + 1], AX.X, ALU.max, negate=True))
        wait(dve, made, shift_read.get(before(n, qb, 1)))
        for part in range(PARTS):
            made = stage("dve_shift").done(dve.tensor_copy(shift16[:, :, part, :], shift[:]))
            if part < PARTS - 1:
                wait(dve, made)
                wait(dve, stage("dve_shift").done(dve.tensor_tensor(
                    shift[:], shift[:], shift16[:, :, part, :], ALU.subtract)))
        split_of[n, qb] = made
        yield BLOCK

    split_of = {}

    def make_shift_rows(n, qb):
        unit = max_unit()
        wait(pe, split_of[n, qb])
        tb = unit.bitcast(BF16)[0:PARTS * GROUP, 0:BLOCK]
        for a in range(TPB):
            tr = pe.transpose(tb[:, a * P:(a + 1) * P], shift16[:, a, :, :], e.ident16[:])
        shift_read[n, qb] = stage("pe_shift_t").done(tr)
        rows = shift_t[qb % 2]
        wait(act, shift_read[n, qb], shift_rows.get(before(n, qb, 2)))
        copied = stage("act_shift_t").done(act.copy(rows[:], tb))
        max_read.append(copied)
        wait(sp, copied)
        for part in range(PARTS):
            shift_rows[n, qb] = shift_in[qb % 2].done(sp.dma_start(
                q_stack[n % STACKS][SLOT_ROWS + part:SLOT_ROWS + part + 1, :, qb * BLOCK:(qb + 1) * BLOCK],
                rows[part * GROUP:(part + 1) * GROUP, :]))

    cost_done = 0

    def all_maxima():
        nonlocal cost_done
        last = None
        for n in range(ALL_GROUPS):
            for qb in range(BLOCKS):
                for product_at, cost in enumerate(find_maxima(n, qb)):
                    if product_at == SHIFT_LAG and last is not None:
                        make_shift_rows(*last)
                        cost += BLOCK
                    cost_done += cost
                    yield cost
                last = (n, qb)
        make_shift_rows(*last)
        yield BLOCK

    unit_free = []
    exp_of, probs_read = {}, {}
    o_copied = []
    norm_of = []

    def next_unit():
        u = len(unit_free)
        if u >= SCORE_BANKS:
            wait(pe, unit_free[u - SCORE_BANKS])
        return bank(u % SCORE_BANKS)

    def attend(n, qb, kt, step):
        off = max(0, kt * P - qb * BLOCK)
        first, last = kt == (qb + 1) * TPB - 1, kt == 0
        b, g = divmod(n, GROUPS)
        for j in range(GROUP):
            wait(pe, *exp_of[step, j])
        if first and o_copied:
            wait(pe, o_copied[-1])
        for j in range(GROUP):
            col = (g * GROUP + j) * V_STRIDE
            mm = pe.matmul(bank(3)[j * COL_TILE:(j + 1) * COL_TILE, off:BLOCK],
                           v_aug[b][:, kt, col:col + COL_TILE],
                           probs[step % 2 * GROUP + j][:, off:BLOCK],
                           start=first, stop=last, skip_group_check=True)
        probs_read[step] = stage("pe_attn").done(mm)
        if last:
            turn = len(o_copied)
            wait(act, probs_read[step])
            if turn >= 2:
                wait(act, o_turned[turn - 2])
            o_copied.append(stage("act_o").done(act.copy(o_t[turn % 2], bank(3))))

    o_turned = []

    def turn_output(n, qb):
        b, g = divmod(n, GROUPS)
        turn = len(o_turned)
        unit = next_unit()
        wait(pe, o_copied[turn])
        for a in range(TPB):
            tr = pe.transpose(unit[:, a * P:(a + 1) * P], o_t[turn % 2][:, a * P:(a + 1) * P], e.ident[:])
        o_turned.append(stage("pe_o").done(tr))
        wait(dve, o_turned[turn])
        heads = unit.rearrange("p (n d) -> p n d", d=COL_TILE)
        rc = recip[turn % 2]
        wait(dve, stage("dve_norm").done(dve.reciprocal(rc[:], heads[:, :, DH])))
        tile0 = b * TILES + qb * TPB
        norm_of.append(stage("dve_norm").done(dve.tensor_tensor(
            e.tokens[:, tile0:tile0 + TPB, g * GROUP * DH:(g + 1) * GROUP * DH]
            .rearrange("p n (h d) -> p n h d", d=DH),
            heads[:, :, 0:DH].rearrange("p (n h) d -> p n h d", n=TPB),
            rc[:].rearrange("p (n h) -> p n h", n=TPB).unsqueeze(3).to_broadcast([P, TPB, GROUP, DH]),
            ALU.mult)))
        unit_free.append(norm_of[-1])
        if g == GROUPS - 1:
            e.block_attended[b * BLOCKS + qb] = norm_of[-1]

    steps = [(n, qb, kt) for n in range(ALL_GROUPS) for qb in range(BLOCKS)
             for kt in reversed(range((qb + 1) * TPB))]
    steps_of_group = len(steps) // ALL_GROUPS

    def score(step, side_work):
        n, qb, kt = steps[step]
        off = max(0, kt * P - qb * BLOCK)
        qs, ks = q_stack[n % STACKS], k_stack[n % STACKS]
        for j in range(GROUP):
            unit = next_unit()
            mm = pe.matmul(unit[:, off:BLOCK], ks[0:SCORE_ROWS, j, kt * P:(kt + 1) * P],
                           qs[0:SCORE_ROWS, j, qb * BLOCK + off:(qb + 1) * BLOCK], start=True, stop=True)
            scored = stage("pe_score").done(mm)
            pr = probs[step % 2 * GROUP + j]
            wait(act, scored, probs_read.get(step - 2))
            exp_done = stage("act_exp").done(act.activation(
                pr[:, off:BLOCK], unit[:, off:BLOCK], ACT.Exp, scale=SOFTMAX_SCALE))
            unit_free.append(exp_done)
            exp_of[step, j] = (exp_done,)
            if kt >= qb * TPB:
                wait(pool, exp_done)
                exp_of[step, j] = (stage("pool_causal").done(pool.affine_select(
                    out=pr[:, off:off + P], in_=pr[:, off:off + P], pattern=[[1, P]],
                    compare_op=ALU.is_ge, fill=0.0, base=0, channel_multiplier=-1)),)
            side_work(BLOCK - off)
        return scored

    wait(pool, proj_in)
    for i in range(TILES + drain):
        projection_step(i)
    wait(sp, ones_made)
    load_stack(0, parts_written[-2:])
    maxima = all_maxima()
    for i in range(TILES + drain, ALL_TILES + drain):
        projection_step(i, maxima if i >= TILES + drain + PROJ_AHEAD else iter(()))
    projected = (bias_of[ALL_TILES - 1], evac_of[ALL_TILES - 1], part_of[ALL_TILES - 1])
    load_stack(1, parts_written[-2:])
    proj.close()
    make_stack(2, early, "left")
    wait(pe, *projected)
    wait(sp, *projected)
    load_stack(2, ())

    slots = [BLOCK - max(0, kt * P - qb * BLOCK) for _, qb, kt in steps for _ in range(GROUP)]
    group_cost = (GROUP * sum((i + 1) * P + (i // TPB + 1) * REDUCE_COST for i in range(TILES))
                  + 2 * BLOCKS * BLOCK)

    def pace_from(n):
        if n < EARLY_GROUPS:
            return EARLY_PACE * group_cost / sum(slots[:steps_of_group * GROUP])
        return (group_cost * (ALL_GROUPS - 1 + MAX_SHARE) - cost_done) / sum(
            slots[n * steps_of_group * GROUP:(ALL_GROUPS - 1) * steps_of_group * GROUP])

    owed = 0.0
    side = maxima

    def last_side_work():
        yield from maxima
        wait(pe, *max_read[-MAX_BANKS:])
        yield from e.experts.beside_attention()

    def side_work(columns):
        nonlocal owed
        owed += columns * pace
        while owed > 0:
            owed -= next(side, BLOCK)

    for step, (n, qb, kt) in enumerate(steps):
        if step % steps_of_group == 0:
            if n < ALL_GROUPS - 1:
                pace = pace_from(n)
            if 0 < n < ALL_GROUPS - STACKS + 1:
                load_stack(n + STACKS - 1, ())
            if n == ALL_GROUPS - 1:
                while (n, 0) not in shift_rows:
                    next(maxima)
                early.close()
                e.experts = ExpertLayer(e, late, stack_free[n - 1])
                side = last_side_work()
                pace = SIDE_PACE * ((1 - MAX_SHARE) * group_cost + e.experts.cost_beside_attention()) / sum(
                    slots[-steps_of_group * GROUP:])
        while steps[min(step + SHIFTS_AHEAD, len(steps) - 1)][:2] not in shift_rows:
            next(maxima)
        if kt == (qb + 1) * TPB - 1:
            wait(pe, shift_rows[n, qb])
        scored = score(step, side_work)
        if step >= 1:
            attend(*steps[step - 1], step - 1)
            if len(o_turned) < len(o_copied) and step >= 2 and steps[step - 2][2] == 0:
                turn_output(*steps[step - 2][:2])
        if step % steps_of_group == steps_of_group - 1:
            stack_free[n] = (scored,)
    attend(*steps[-1], len(steps) - 1)
    turn_output(*steps[-1][:2])
    while 0 not in e.experts.combined_of:
        next(side)
    e.attended = (norm_of[-1], probs_read[len(steps) - 1], exp_of[len(steps) - 1, GROUP - 1][0])


def product(pe, out, lhs, rhs, start=True, stop=True):
    pe.matmul(out, lhs[0], rhs[0], start=start, stop=False)
    pe.matmul(out, lhs[0], rhs[1], start=False, stop=False)
    return pe.matmul(out, lhs[1], rhs[0], start=False, stop=stop)


class ExpertLayer:

    WEIGHTS = (("w_out", (CHUNKS, DIM)), ("w_router", (CHUNKS, EXPERTS)),
               ("w_gate", (CHUNKS, ALL_EXPERTS * INTER)), ("w_up", (CHUNKS, ALL_EXPERTS * INTER)),
               ("w_down", (ALL_EXPERTS, DIM)))
    PIECE = ALL_EXPERTS * INTER

    def __init__(self, e, room, room_free):
        self.e, self.room = e, room
        self.x_res = [self.sbuf(f"x_res{i}", [P, TPB, DIM]) for i in range(2)]
        self.high, self.low, self.ready = {}, {}, {}
        for name, shape in self.WEIGHTS:
            self.high[name] = self.sbuf(name + "_high", [P, *shape], F32R)
            self.low[name] = self.sbuf(name + "_low", [P, *shape], F32R)
        self.raw = [self.sbuf(f"w_raw{i}", [P, self.PIECE]) for i in range(2)]
        self.attn_high = [self.sbuf(f"attn_high{i}", [P, CHUNKS, P], F32R) for i in range(2)]
        self.attn_low = [self.sbuf(f"attn_low{i}", [P, CHUNKS, P], F32R) for i in range(2)]
        self.stats = self.sbuf("stats", [P, ALL_TILES, 6])
        self.mean_var = self.sbuf("mean_var", [P, ALL_TILES, 2])
        self.rstd = self.sbuf("rstd", [P, ALL_TILES])
        self.x1_high = [self.sbuf("x1_high0", [P, CHUNKS, BLOCK], F32R)]
        self.x1_low = [self.sbuf("x1_low0", [P, CHUNKS, BLOCK], F32R)]
        self.small = {name: self.sbuf("router_" + name, [P, TPB, EXPERTS], U32 if name == "top_at" else F32)
                      for name in ("score", "top", "top_at", "top_atf", "pick", "pick2")}
        self.logits_t = self.sbuf("logits_t", [EXPERTS, BLOCK])
        self.logits_turned = None
        self.row_stat = self.sbuf("row_stat", [P, TPB])
        self.combine = [self.sbuf(f"combine{i}", [P, TPB, EXPERTS]) for i in range(2)]

        self.turned_of, self.high_of, self.low_of, self.res_of, self.out_of = {}, {}, {}, {}, {}
        self.biased_of, self.x_marks, self.known_of, self.ln1_of = {}, {}, {}, {}
        self.combined_of, self.x1_of, self.bank7_read = {}, {}, None
        self.h_of, self.low_h_of, self.silu_of, self.up_of, self.down_of, self.y_of = {}, {}, {}, {}, {}, {}
        self.x_in = [e.dma_stage(f"x_in{i}") for i in range(2)]
        self.raw_in = [e.dma_stage(f"w_raw_in{i}") for i in range(2)]
        for engine in (e.nc.sync, e.nc.vector, e.nc.scalar, e.nc.gpsimd):
            wait(engine, *room_free)
        self.b_out_in = e.dma_stage("b_out_in").done(e.nc.sync.dma_start(e.b_out[:], e.t["b_out"]))
        self.load_x(0)
        self.weights = self.split_weights()
        advance(self.weights)
        self.rest = self.add_attention(TILES, TILES)
        self.load_x(1)

    def sbuf(self, name, shape, dtype=F32):
        return self.e.sbuf(name, shape, dtype, self.room)

    def load_x(self, blk):
        e = self.e
        self.x_marks[blk] = self.x_in[blk % 2].done(e.nc.sync.dma_start(
            self.x_res[blk % 2][:],
            e.t["x"][blk * BLOCK:(blk + 1) * BLOCK, :].rearrange("(n p) c -> p n c", p=P)))

    def split_weights(self):
        e, dve, sp = self.e, self.e.nc.vector, self.e.nc.sync
        pieces = []
        for name, (n, m) in self.WEIGHTS:
            flat = [buf[:].rearrange("p n m -> p (n m)") for buf in (self.high[name], self.low[name])]
            src = e.t[name].rearrange("p n m -> p (n m)")
            for at in range(0, n * m, self.PIECE):
                cols = slice(at, min(at + self.PIECE, n * m))
                pieces.append((name, src[:, cols], flat[0][:, cols], flat[1][:, cols], cols.stop - at))
        done, loaded = [], []

        def load(k):
            if k < len(pieces):
                if k >= 2:
                    wait(sp, done[k - 2])
                loaded.append(self.raw_in[k % 2].done(
                    sp.dma_start(self.raw[k % 2][:, 0:pieces[k][4]], pieces[k][1])))

        load(0)
        load(1)
        yield 0
        for k, (name, _, high, low, width) in enumerate(pieces):
            raw = self.raw[k % 2][:, 0:width]
            wait(dve, loaded[k])
            wait(dve, e.stage("dve_w_high").done(dve.tensor_copy(high, raw)))
            done.append(e.stage("dve_w_low").done(dve.tensor_tensor(low, raw, high, ALU.subtract)))
            self.ready[name] = done[k]
            load(k + 2)
            yield self.PIECE + self.PIECE // 2

    def turn_attention(self, i):
        e, pe, act, dve = self.e, self.e.nc.tensor, self.e.nc.scalar, self.e.nc.vector
        blk, at = divmod(i, TPB)
        buf = i % 2
        rounder, adder = self.rounder, self.adder
        if at == 0 and blk >= 2:
            wait(e.nc.sync, self.res_of[(blk - 1) * TPB - 1])
            self.load_x(blk)
        wait(adder, self.x_marks[blk], self.b_out_in)
        name = "dve_bias" if adder is dve else "pool_bias"
        self.biased_of[i] = e.stage(name).done(adder.tensor_tensor(
            self.x_res[blk % 2][:, at, :], self.x_res[blk % 2][:, at, :], e.b_out[:], ALU.add))
        wait(pe, self.bank7_read, e.block_attended[blk])
        for c in range(CHUNKS):
            tr = pe.transpose(e.bank(7)[:, c * P:(c + 1) * P], e.tokens[:, i, c * P:(c + 1) * P], e.ident[:])
        turned = e.stage("pe_attn_t").done(tr)
        src = e.bank(7)[:, 0:DIM].rearrange("p (c q) -> p c q", c=CHUNKS)
        wait(rounder, turned, self.out_of.get(i - 2))
        if rounder is dve:
            rounded = e.stage("dve_attn_high").done(dve.tensor_copy(self.attn_high[buf][:], src))
        else:
            rounded = e.stage("act_attn_high").done(act.copy(self.attn_high[buf][:], src))
        wait(dve, rounded, self.out_of.get(i - 2))
        self.bank7_read = self.low_of[i] = e.stage("dve_attn_low").done(
            dve.tensor_tensor(self.attn_low[buf][:], src, self.attn_high[buf][:], ALU.subtract))

    def output_product(self, i):
        e, pe, dve = self.e, self.e.nc.tensor, self.e.nc.vector
        blk, at = divmod(i, TPB)
        buf = i % 2
        wait(pe, self.low_of[i], self.res_of.get(i - 1), self.ready["w_out"])
        for c in range(CHUNKS):
            mm = product(pe, e.bank(6)[:, 0:DIM], (self.attn_high[buf][:, c, :], self.attn_low[buf][:, c, :]),
                         (self.high["w_out"][:, c, :], self.low["w_out"][:, c, :]), c == 0, c == CHUNKS - 1)
        self.out_of[i] = e.stage("pe_out").done(mm)
        wait(dve, self.out_of[i], self.biased_of[i])
        self.res_of[i] = e.stage("dve_res").done(dve.tensor_tensor(
            e.tokens[:, i, :], e.bank(6)[:, 0:DIM], self.x_res[blk % 2][:, at, :], ALU.add))
        wait(dve, self.res_of[i])
        self.statistics(i)

    def statistics(self, i):
        e, dve = self.e, self.e.nc.vector
        wait(dve, e.stage("dve_ln").done(dve.bn_stats(self.stats[:, i, :], e.tokens[:, i, :])))
        self.known_of[i] = e.stage("dve_ln").done(dve.bn_aggr(self.mean_var[:, i, :], self.stats[:, i, :]))

    def inverse_deviation(self, first, n, pause=0):
        e, act, dve = self.e, self.e.nc.scalar, self.e.nc.vector
        tiles = slice(first, first + n)
        wait(act, self.known_of[first + n - 1], e.consts)
        root = e.stage("act_sqrt").done(act.activation(self.rstd[:, tiles], self.mean_var[:, tiles, 1], ACT.Sqrt,
                                                       bias=e.eps[:]))
        yield pause
        wait(dve, root)
        wait(dve, e.stage("dve_ln").done(dve.reciprocal(self.rstd[:, tiles], self.rstd[:, tiles])))

    def normalise(self, i):
        e = self.e
        return e.stage("dve_ln").done(e.nc.vector.tensor_scalar(
            e.tokens[:, i, :], e.tokens[:, i, :], self.mean_var[:, i, 0:1], self.rstd[:, i:i + 1],
            ALU.subtract, ALU.mult))

    def add_attention(self, first, n):
        for i in range(first, first + n + 1):
            if i < first + n:
                self.turn_attention(i)
                yield TURN_COST
            if i > first:
                self.output_product(i - 1)
                yield PRODUCT_COST

    def normalise_tiles(self, first, n, pause=0):
        yield pause
        yield from self.inverse_deviation(first, n, pause)
        for i in range(first, first + n):
            self.ln1_of[i] = self.normalise(i)
            if i % TPB == TPB - 1:
                yield pause

    def prepare(self, blk):
        e, bank = self.e, self.e.bank
        pe, act, dve = e.nc.tensor, e.nc.scalar, e.nc.vector
        half = blk % 2
        x1_high, x1_low = self.x1_high[half], self.x1_low[half]
        if blk >= 2:
            last_read = self.up_of[(blk - 1) * ALL_EXPERTS - 1]
            wait(act, last_read)
            wait(dve, last_read)
        for a in range(TPB):
            i = blk * TPB + a
            wait(pe, self.ln1_of[i], self.bank7_read)
            for c in range(CHUNKS):
                tr = pe.transpose(bank(7)[:, c * P:(c + 1) * P], e.tokens[:, i, c * P:(c + 1) * P], e.ident[:])
            wait(self.rounder, e.stage("pe_x1_t").done(tr))
            src = bank(7)[:, 0:DIM].rearrange("p (c q) -> p c q", c=CHUNKS)
            if self.rounder is dve:
                rounded = e.stage("dve_x1_high").done(dve.tensor_copy(x1_high[:, :, a * P:(a + 1) * P], src))
            else:
                rounded = e.stage("act_x1_high").done(act.copy(x1_high[:, :, a * P:(a + 1) * P], src))
            wait(dve, rounded)
            self.bank7_read = self.x1_of[i] = e.stage("dve_x1_low").done(dve.tensor_tensor(
                x1_low[:, :, a * P:(a + 1) * P], src, x1_high[:, :, a * P:(a + 1) * P], ALU.subtract))
            yield DIM
        wait(pe, self.bank7_read, self.ready["w_router"])
        for c in range(CHUNKS):
            mm = product(pe, bank(7)[0:EXPERTS, :], (self.high["w_router"][:, c, :], self.low["w_router"][:, c, :]),
                         (x1_high[:, c, :], x1_low[:, c, :]), c == 0, c == CHUNKS - 1)
        wait(act, e.stage("pe_router").done(mm), self.logits_turned)
        copied = self.bank7_read = e.stage("act_logits").done(act.copy(self.logits_t[:], bank(7)[0:EXPERTS, :]))
        yield BLOCK
        logits = bank(7)[:, 0:TPB * EXPERTS].rearrange("p (n k) -> p n k", k=EXPERTS)
        wait(pe, copied, self.bank7_read)
        for a in range(TPB):
            tr = pe.transpose(logits[:, a, :], self.logits_t[:, a * P:(a + 1) * P],
                              e.ident[0:EXPERTS, 0:EXPERTS])
        scored = self.logits_turned = e.stage("pe_logits_t").done(tr)

        def over_experts(ap):
            return ap.unsqueeze(2).to_broadcast([P, TPB, EXPERTS])

        r = e.stage("dve_router")
        v = {name: buf[:] for name, buf in self.small.items()}
        total = self.row_stat[:]
        wait(dve, scored)
        wait(dve, r.done(dve.tensor_reduce(total, logits, AX.X, ALU.max)))
        self.bank7_read = r.done(dve.tensor_tensor(v["score"], logits, over_experts(total), ALU.subtract))
        wait(act, self.bank7_read)
        powers = e.stage("act_router").done(act.activation(v["score"], v["score"], ACT.Exp))
        yield BLOCK
        wait(dve, powers)
        wait(dve, r.done(dve.tensor_reduce(total, v["score"], AX.X, ALU.add)))
        wait(dve, r.done(dve.reciprocal(total, total)))
        wait(dve, r.done(dve.tensor_tensor(v["score"], v["score"], over_experts(total), ALU.mult)))
        yield 0
        for a in range(TPB):
            m = r.done(dve.max(v["top"][:, a, :], v["score"][:, a, :]))
        wait(dve, m)
        for a in range(TPB):
            m = r.done(dve.max_index(v["top_at"][:, a, :], v["top"][:, a, :], v["score"][:, a, :]))
        wait(dve, m)
        yield 0
        wait(dve, r.done(dve.tensor_copy(v["top_atf"], v["top_at"])))
        ids = e.expert_ids[:].unsqueeze(1).to_broadcast([P, TPB, EXPERTS])
        wait(dve, e.consts)
        for k, dst in ((0, v["pick"]), (1, v["pick2"])):
            m = r.done(dve.tensor_tensor(dst, ids, over_experts(v["top_atf"][:, :, k]), ALU.is_equal))
        wait(dve, m)
        wait(dve, r.done(dve.tensor_tensor(v["pick"], v["pick"], v["pick2"], ALU.add)))
        self.combined_of[blk] = r.done(dve.tensor_tensor(self.combine[half][:], v["pick"], v["score"], ALU.mult))
        yield 0

    def gate_up(self, n, after_gate, after_up):
        e, bank, high, low = self.e, self.e.bank, self.high, self.low
        pe, act, dve, pool = e.nc.tensor, e.nc.scalar, e.nc.vector, e.nc.gpsimd
        blk, k = self.jobs[n]
        buf, half = n % 2, blk % 2
        cols = slice(k * INTER, (k + 1) * INTER)
        wait(pe, self.h_of.get(n - 2), self.x1_of[blk * TPB + TPB - 1])
        for dst, name in ((bank(buf), "w_gate"), (bank(2 + buf), "w_up")):
            wait(pe, self.ready[name])
            for c in range(CHUNKS):
                mm = product(pe, dst, (high[name][:, c, cols], low[name][:, c, cols]),
                             (self.x1_high[half][:, c, :], self.x1_low[half][:, c, :]),
                             c == 0, c == CHUNKS - 1)
            if name == "w_gate":
                wait(act, e.stage("pe_gate").done(mm), self.h_of.get(n - 2))
                self.silu_of[n] = e.stage("act_silu").done(
                    act.activation(self.silu[buf][:], bank(buf), ACT.Silu))
                for side in after_gate:
                    advance(side)
        self.up_of[n] = e.stage("pe_up").done(mm)
        advance(after_up)
        wait(dve, self.up_of[n], self.silu_of[n], self.low_h_of.get(n - 2))
        self.h_of[n] = e.stage("dve_h").done(dve.tensor_tensor(
            self.hidden[buf][:], bank(2 + buf), self.silu[buf][:], ALU.mult))
        wait(act, self.h_of[n], self.down_of.get(n - 2))
        rounded = e.stage("act_h_high").done(act.copy(self.hid_high[buf][:], self.hidden[buf][:]))
        wait(pool, rounded, self.down_of.get(n - 2))
        self.low_h_of[n] = e.stage("pool_h_low").done(pool.tensor_tensor(
            self.hid_low[buf][:], self.hidden[buf][:], self.hid_high[buf][:], ALU.subtract))

    def down(self, n):
        e, pe, dve, tokens = self.e, self.e.nc.tensor, self.e.nc.vector, self.e.tokens
        blk, k = self.jobs[n]
        buf = n % 2
        wait(pe, self.low_h_of[n], self.ready["w_down"])
        for pair in range(TPB // 2):
            wait(pe, self.y_of.get((n - 1, pair)))
            for a in range(2):
                at = slice((pair * 2 + a) * P, (pair * 2 + a + 1) * P)
                mm = product(pe, e.bank(4 + pair)[:, a * DIM:(a + 1) * DIM],
                             (self.hid_high[buf][:, at], self.hid_low[buf][:, at]),
                             (self.high["w_down"][:, k, :], self.low["w_down"][:, k, :]))
            self.down_of[n] = e.stage("pe_down").done(mm)
            wait(dve, self.down_of[n], self.y_of.get((n - 1, pair)))
            if k == 1:
                wait(dve, self.combined_of[blk])
            for a in range(2):
                i = blk * TPB + pair * 2 + a
                y = e.bank(4 + pair)[:, a * DIM:(a + 1) * DIM]
                if k == 0:
                    op = dve.tensor_tensor(tokens[:, i, :], y, tokens[:, i, :], ALU.add)
                else:
                    op = dve.scalar_tensor_tensor(
                        out=tokens[:, i, :], in0=y,
                        scalar=self.combine[blk % 2][:, pair * 2 + a, k - 1:k],
                        in1=tokens[:, i, :], op0=ALU.mult, op1=ALU.add)
            self.y_of[n, pair] = e.stage("dve_y").done(op)

    def finish(self, blk):
        e, dve, sp = self.e, self.e.nc.vector, self.e.nc.sync
        first = blk * TPB
        wait(dve, self.y_of[(blk + 1) * ALL_EXPERTS - 1, TPB // 2 - 1])
        for i in range(first, first + TPB):
            self.statistics(i)
            yield 0
        yield from self.inverse_deviation(first, TPB)
        for i in range(first, first + TPB, 2):
            self.normalise(i)
            wait(sp, self.normalise(i + 1))
            self.stores.append(e.dma_stage(f"y_out{i // 2}").done(sp.dma_start(
                e.t["out"][i * P:(i + 2) * P, :].rearrange("(n p) c -> p n c", p=P), e.tokens[:, i:i + 2, :])))
        yield 0

    def beside_attention(self):
        dve = self.e.nc.vector
        advance(self.weights, 2)
        self.rounder = self.adder = dve
        for step, cost in enumerate(self.add_attention(0, TILES)):
            yield cost
            if step % 3 == 2:
                yield next(self.weights, 0)
        yield from self.weights
        yield from self.normalise_tiles(0, TILES, 2 * BLOCK)
        for cost in self.prepare(0):
            yield max(cost, BLOCK)
        while True:
            if len(self.low_of) // TPB in self.e.block_attended:
                yield next(self.rest)
            else:
                yield BLOCK

    def cost_beside_attention(self):
        return (TILES * (TURN_COST + PRODUCT_COST) + (2 * (2 + BLOCKS) + 2 * TPB) * BLOCK
                + ALL_EXPERTS * self.PIECE)

    def after_attention(self):
        e = self.e
        pe, act, dve, pool, sp = e.nc.tensor, e.nc.scalar, e.nc.vector, e.nc.gpsimd, e.nc.sync
        self.x1_high.append(self.sbuf("x1_high1", [P, CHUNKS, BLOCK], F32R))
        self.x1_low.append(self.sbuf("x1_low1", [P, CHUNKS, BLOCK], F32R))
        self.silu = [self.sbuf(f"silu{i}", [P, BLOCK]) for i in range(2)]
        self.hidden = [self.sbuf(f"hidden{i}", [P, BLOCK]) for i in range(2)]
        self.hid_high = [self.sbuf(f"hid_high{i}", [P, BLOCK], F32R) for i in range(2)]
        self.hid_low = [self.sbuf(f"hid_low{i}", [P, BLOCK], F32R) for i in range(2)]
        self.stores = []
        for engine in (pe, act, dve, pool, sp):
            wait(engine, *e.attended)

        self.rounder, self.adder = act, pool
        rest = self.rest
        self.jobs = [(blk, k) for blk in range(ALL_BLOCKS) for k in range(ALL_EXPERTS)]
        normalising = finishing = iter(())
        for n, (blk, k) in enumerate(self.jobs):
            if k == 0 and blk + 1 < ALL_BLOCKS:
                for _ in normalising:
                    pass
                preparing = self.prepare(blk + 1)
            if k == NORMALISE_AT and BLOCKS <= blk + 2 < ALL_BLOCKS:
                while (blk + 3) * TPB - 1 not in self.known_of:
                    advance(rest)
                normalising = self.normalise_tiles((blk + 2) * TPB, TPB)
            self.gate_up(n, (preparing, normalising, finishing), rest)
            if n >= 1:
                self.down(n - 1)
                if k == 0:
                    finishing = self.finish(blk - 1)
        for _ in chain(rest, preparing, finishing):
            pass
        self.down(len(self.jobs) - 1)
        advance(self.finish(ALL_BLOCKS - 1), 99)

        wait(sp, *self.stores)


def rotation_tables():
    f = np.float32
    pos = np.arange(SEQ, dtype=f)
    inv_freq = (f(1.0) / f(10000.0) ** (np.arange(0, DH, 2, dtype=f) / f(DH))).astype(f)
    freqs = np.repeat(pos[:, None] * inv_freq[None, :], 2, axis=-1)
    cos, sin = np.cos(freqs), np.sin(freqs)
    base = (np.arange(0, DH, 2, dtype=f) + f(0.4 * DH)) / f(1.4 * DH)
    power = (pos - f(SEQ // 2)) / f(512.0)
    scale = base[None, :] ** power[:, None]
    scale = np.concatenate((scale, scale), axis=-1).astype(f)
    sign = np.where(np.arange(DH) % 2 == 0, f(-1.0), f(1.0))[None, :]
    both = np.stack((scale, f(1.0) / scale), axis=1)
    cos_t, sin_t = cos[:, None, :] * both, (sin * sign)[:, None, :] * both

    def tiled(a):
        return np.ascontiguousarray(a.reshape(TILES, P, 2, DH).transpose(1, 0, 2, 3).astype(f))

    return tiled(cos_t), tiled(sin_t)


def kernel(L0_attn_x, L0_attn_Wq, L0_attn_bq, L0_attn_Wk, L0_attn_bk, L0_attn_Wv, L0_attn_bv,
           L0_attn_Wo, L0_attn_bo, L0_ffn_gate_w, L0_ffn_wg, L0_ffn_wu, L0_ffn_wd, L0_ffn_sg,
           L0_ffn_su, L0_ffn_sd):
    import concourse.bacc as bacc
    from concourse.bass_utils import run_bass_kernel_spmd

    def chunked(w):
        return w.reshape(-1, P, w.shape[-1]).transpose(1, 0, 2)

    def rows(v):
        return np.broadcast_to(v[None, :], (P, v.shape[0]))

    x = np.asarray(L0_attn_x).reshape(BATCH * SEQ, DIM)
    w_qkv = np.concatenate([np.asarray(w).T for w in (L0_attn_Wq, L0_attn_Wv, L0_attn_Wk)], axis=1)
    b_qkv = np.concatenate([np.asarray(v) for v in (L0_attn_bq, L0_attn_bv, L0_attn_bk)])
    gate = np.concatenate([np.asarray(L0_ffn_sg)[None], np.asarray(L0_ffn_wg)]).reshape(-1, DIM).T
    up = np.concatenate([np.asarray(L0_ffn_su)[None], np.asarray(L0_ffn_wu)]).reshape(-1, DIM).T
    down = np.concatenate([np.asarray(L0_ffn_sd)[None], np.asarray(L0_ffn_wd)]).transpose(2, 0, 1)
    cos_t, sin_t = rotation_tables()
    arrays = {
        "x": x, "x_t": x.T, "w_qkv": chunked(w_qkv), "b_qkv": rows(b_qkv),
        "rot_cos": cos_t, "rot_sin": sin_t, "ident": np.eye(P, dtype=np.float32),
        "w_out": chunked(np.asarray(L0_attn_Wo).T), "b_out": rows(np.asarray(L0_attn_bo)),
        "w_router": chunked(np.asarray(L0_ffn_gate_w).T), "w_gate": chunked(gate),
        "w_up": chunked(up), "w_down": down,
    }
    arrays = {k: np.ascontiguousarray(v) for k, v in arrays.items()}
    nc = bacc.Bacc("TRN2", target_bir_lowering=False, num_devices=1)
    tensors = {k: nc.dram_tensor(k + "_dram", v.shape, mybir.dt.from_np(v.dtype), kind="ExternalInput").ap()
               for k, v in arrays.items()}
    tensors["parts_dram"] = nc.dram_tensor("parts_scratch", (PARTS * 4, P, BATCH * SEQ), BF16, kind="Internal").ap()
    tensors["out"] = nc.dram_tensor("out_dram", (BATCH * SEQ, DIM), F32, kind="ExternalOutput").ap()
    build_program(nc, tensors)
    result = run_bass_kernel_spmd(nc, [{k + "_dram": v for k, v in arrays.items()}], core_ids=[0])
    return result.results[0]["out_dram"].reshape(BATCH, SEQ, DIM)
```
